# Optimizing a Trainium2 kernel written in Bass

```python
import numpy as np
import jax
import jax.numpy as jnp

def _softmax(x, axis=-1):
    return jax.nn.softmax(x, axis=axis)

def _gelu(x):
    return jax.nn.gelu(x, approximate=True)

def _silu(x):
    return jax.nn.silu(x)

def _sigmoid(x):
    return jax.nn.sigmoid(x)

def _layernorm(x, axis=-1, eps=1e-05):
    m = jnp.mean(x, axis=axis, keepdims=True)
    v = jnp.var(x, axis=axis, keepdims=True)
    return (x - m) / jnp.sqrt(v + eps)

def _scatter_add(tgt, idx, src, axis=0):
    return tgt.at[idx].add(src)

def _segment_sum(src, seg, n):
    return jax.ops.segment_sum(src, seg, n)
kernel_name = 'mk_adj_resnorm_d4_adj_r2_fe2d4c'

def setup_inputs(seed: int=0):
    np.random.seed(seed)
    _w = jnp.asarray

    def _rec_inputs():
        import jax
        import jax.numpy as jnp
        _gk = jax.random.key(seed)
        x = -0.0003929 + 0.9999 * jax.random.normal(jax.random.fold_in(_gk, 1), (64, 128, 128), jnp.float32)
        _a = jax.random.bernoulli(jax.random.fold_in(_gk, 2), 0.125, (128, 128))
        _a = jnp.logical_or(_a, jnp.swapaxes(_a, -1, -2))
        _a = jnp.logical_or(_a, jnp.eye(128, dtype=bool))
        _af = _a.astype(jnp.float32)
        _af = _af * jax.random.uniform(jax.random.fold_in(_gk, 3), (128, 128), jnp.float32, 0.05, 0.999963)
        adj = _af
        return (x, adj)
    x, adj = _rec_inputs()

    def _L0_gnn_setup():
        import jax, jax.numpy as jnp
        import numpy as np
        BT, N, D, HEADS, E = (512, 64, 128, 4, 256)
        LRELU_SLOPE = 0.2
        EPS = 1e-08
        key = jax.random.key(seed)
        ks = jax.random.split(key, 8)
        d = D
        return {'H': jax.random.normal(ks[0], (BT, N, d), jnp.float32), 'W_lin': jax.random.normal(ks[1], (d, d), jnp.float32) / np.sqrt(d).astype(np.float32), 'W_val': jax.random.normal(ks[2], (d, d), jnp.float32) / np.sqrt(d).astype(np.float32), 'a': jax.random.normal(ks[3], (HEADS, d // HEADS), jnp.float32), 'W_out': jax.random.normal(ks[4], (d, d), jnp.float32) / np.sqrt(d).astype(np.float32), 'A0': jax.random.uniform(ks[5], (N, N), jnp.float32), 'src': jax.random.randint(ks[6], (E,), 0, N, jnp.int32), 'dst': jax.random.randint(ks[7], (E,), 0, N, jnp.int32)}
    _L0_gnn_all = _L0_gnn_setup()
    _L0_gnn_in = {k: v for k, v in _L0_gnn_all.items() if k in ('W_lin', 'W_val', 'a', 'W_out', 'src', 'dst')}
    del _L0_gnn_all

    def _L1_gnn_setup():
        import jax, jax.numpy as jnp
        import numpy as np
        B, T, D, H = (64, 1024, 128, 128)
        MAX_SKIP = 4

        def _lstm_last(Wih, Whh, bih, bhh, xs):
            N, _, Hd = xs.shape
            bias = bih + bhh

            def step(carry, x_t):
                h, c = carry
                g = x_t @ Wih.T + h @ Whh.T + bias
                i, f, gg, o = jnp.split(g, 4, axis=-1)
                c = jax.nn.sigmoid(f) * c + jax.nn.sigmoid(i) * jnp.tanh(gg)
                h = jax.nn.sigmoid(o) * jnp.tanh(c)
                return ((h, c), None)
            init = (jnp.zeros((N, Hd), xs.dtype), jnp.zeros((N, Hd), xs.dtype))
            (h_last, _), _ = jax.lax.scan(step, init, jnp.swapaxes(xs, 0, 1))
            return h_last
        key = jax.random.key(seed)
        ks = jax.random.split(key, 8)
        s = 0.05
        x = jax.random.normal(ks[0], (B, T, D), jnp.float32)
        adj = jax.random.uniform(ks[1], (T, T), jnp.float32) / T
        Wg0 = jax.random.normal(ks[2], (D, H), jnp.float32) * s
        bg0 = jnp.zeros((H,), jnp.float32)
        Wg1 = jax.random.normal(ks[3], (H, H), jnp.float32) * s
        bg1 = jnp.zeros((H,), jnp.float32)
        Wih = jax.random.normal(ks[4], (MAX_SKIP, 4 * H, H), jnp.float32) * s
        Whh = jax.random.normal(ks[5], (MAX_SKIP, 4 * H, H), jnp.float32) * s
        bih = jax.random.normal(ks[6], (MAX_SKIP, 4 * H), jnp.float32) * s
        bhh = jax.random.normal(ks[7], (MAX_SKIP, 4 * H), jnp.float32) * s
        return dict(x=x, adj=adj, Wg0=Wg0, bg0=bg0, Wg1=Wg1, bg1=bg1, Wih=Wih, Whh=Whh, bih=bih, bhh=bhh)
    _L1_gnn_all = _L1_gnn_setup()
    _L1_gnn_in = {k: v for k, v in _L1_gnn_all.items() if k in ('Wg0', 'bg0', 'Wg1', 'bg1', 'Wih', 'Whh', 'bih', 'bhh')}
    del _L1_gnn_all

    def _L2_gnn_setup():
        import jax, jax.numpy as jnp
        import numpy as np
        N = 3445
        B = 32
        IN_DIM = 128
        HID_DIM = 128

        def _make_adj(key):
            a = jax.random.uniform(key, (N, N), dtype=jnp.float32)
            a = (a < 0.001).astype(jnp.float32)
            a = jnp.maximum(a, a.T)
            deg = jnp.sum(a, axis=1, keepdims=True)
            return a / jnp.maximum(deg, 1.0)

        def _graph_conv(x, adj, w_loop, w_neigh, b):
            loop = jnp.einsum('bnd,dh->bnh', x, w_loop)
            neigh = jnp.einsum('nm,bmh->bnh', adj, jnp.einsum('bnd,dh->bnh', x, w_neigh))
            return loop + neigh + b
        key = jax.random.key(seed)
        k = jax.random.split(key, 8)
        s1 = 1.0 / np.sqrt(IN_DIM)
        s2 = 1.0 / np.sqrt(HID_DIM)
        return {'x': jax.random.normal(k[0], (B, N, IN_DIM), dtype=jnp.float32), 'adj': _make_adj(k[1]), 'w1_loop': jax.random.normal(k[2], (IN_DIM, HID_DIM), dtype=jnp.float32) * s1, 'w1_neigh': jax.random.normal(k[3], (IN_DIM, HID_DIM), dtype=jnp.float32) * s1, 'b1': jnp.zeros((HID_DIM,), dtype=jnp.float32), 'w2_loop': jax.random.normal(k[4], (HID_DIM, IN_DIM), dtype=jnp.float32) * s2, 'w2_neigh': jax.random.normal(k[5], (HID_DIM, IN_DIM), dtype=jnp.float32) * s2, 'b2': jnp.zeros((IN_DIM,), dtype=jnp.float32)}
    _L2_gnn_all = _L2_gnn_setup()
    _L2_gnn_in = {k: v for k, v in _L2_gnn_all.items() if k in ('w1_loop', 'w1_neigh', 'b1', 'w2_loop', 'w2_neigh', 'b2')}
    del _L2_gnn_all

    def _L3_gnn_setup():
        import jax, jax.numpy as jnp
        import numpy as np
        NEG = -1e+30
        key = jax.random.key(seed)
        ks = jax.random.split(key, 4)
        B, T, C = (4, 2048, 128)
        x = jax.random.normal(ks[0], (B, T, C), dtype=jnp.float32)
        adj_mask = jax.random.normal(ks[1], (T, T), dtype=jnp.float32)
        Wqkv = jax.random.normal(ks[2], (C, 3 * C), dtype=jnp.float32) * (1.0 / np.sqrt(C))
        Wo = jax.random.normal(ks[3], (C, C), dtype=jnp.float32) * (1.0 / np.sqrt(C))
        return {'x': x, 'adj_mask': adj_mask, 'Wqkv': Wqkv, 'Wo': Wo}
    _L3_gnn_all = _L3_gnn_setup()
    _L3_gnn_in = {k: v for k, v in _L3_gnn_all.items() if k in ('Wqkv', 'Wo')}
    del _L3_gnn_all
    return {'x': x, 'adj': adj, 'L0_gnn_W_lin': _L0_gnn_in['W_lin'], 'L0_gnn_W_val': _L0_gnn_in['W_val'], 'L0_gnn_a': _L0_gnn_in['a'], 'L0_gnn_W_out': _L0_gnn_in['W_out'], 'L0_gnn_src': _L0_gnn_in['src'], 'L0_gnn_dst': _L0_gnn_in['dst'], 'L1_gnn_Wg0': _L1_gnn_in['Wg0'], 'L1_gnn_bg0': _L1_gnn_in['bg0'], 'L1_gnn_Wg1': _L1_gnn_in['Wg1'], 'L1_gnn_bg1': _L1_gnn_in['bg1'], 'L1_gnn_Wih': _L1_gnn_in['Wih'], 'L1_gnn_Whh': _L1_gnn_in['Whh'], 'L1_gnn_bih': _L1_gnn_in['bih'], 'L1_gnn_bhh': _L1_gnn_in['bhh'], 'L2_gnn_w1_loop': _L2_gnn_in['w1_loop'], 'L2_gnn_w1_neigh': _L2_gnn_in['w1_neigh'], 'L2_gnn_b1': _L2_gnn_in['b1'], 'L2_gnn_w2_loop': _L2_gnn_in['w2_loop'], 'L2_gnn_w2_neigh': _L2_gnn_in['w2_neigh'], 'L2_gnn_b2': _L2_gnn_in['b2'], 'L3_gnn_Wqkv': _L3_gnn_in['Wqkv'], 'L3_gnn_Wo': _L3_gnn_in['Wo']}

def reference(x, adj, L0_gnn_W_lin, L0_gnn_W_val, L0_gnn_a, L0_gnn_W_out, L0_gnn_src, L0_gnn_dst, L1_gnn_Wg0, L1_gnn_bg0, L1_gnn_Wg1, L1_gnn_bg1, L1_gnn_Wih, L1_gnn_Whh, L1_gnn_bih, L1_gnn_bhh, L2_gnn_w1_loop, L2_gnn_w1_neigh, L2_gnn_b1, L2_gnn_w2_loop, L2_gnn_w2_neigh, L2_gnn_b2, L3_gnn_Wqkv, L3_gnn_Wo):
    import jax
    import jax.numpy as jnp

    def _L0_gnn_ref(H, W_lin, W_val, a, W_out, A0, src, dst):
        import jax, jax.numpy as jnp
        import numpy as np
        BT, N, D, HEADS, E = (512, 64, 128, 4, 256)
        LRELU_SLOPE = 0.2
        EPS = 1e-08
        bt, n, d = H.shape
        h, dh = a.shape
        Xq = (H @ W_lin.T).reshape(bt, n, h, dh)
        Xv = (H @ W_val.T).reshape(bt, n, h, dh)
        Qs = Xq[:, src]
        Kt = Xq[:, dst]
        e = jnp.einsum('behd,hd->beh', jax.nn.leaky_relu(Qs + Kt, LRELU_SLOPE), a)
        e = e + jnp.log(A0[src, dst] + EPS)[None, :, None]
        e_t = e.transpose(1, 0, 2)
        m = jax.ops.segment_max(e_t, src, num_segments=n)
        ex = jnp.exp(e_t - m[src])
        denom = jax.ops.segment_sum(ex, src, num_segments=n)
        attn = ex / denom[src]
        Vt = Xv[:, dst].transpose(1, 0, 2, 3)
        Y = jax.ops.segment_sum(attn[..., None] * Vt, src, num_segments=n)
        Y = Y.transpose(1, 0, 2, 3).reshape(bt, n, d)
        return Y @ W_out.T

    def _L1_gnn_ref(x, adj, Wg0, bg0, Wg1, bg1, Wih, Whh, bih, bhh):
        import jax, jax.numpy as jnp
        import numpy as np
        B, T, D, H = (64, 1024, 128, 128)
        MAX_SKIP = 4

        def _lstm_last(Wih, Whh, bih, bhh, xs):
            N, _, Hd = xs.shape
            bias = bih + bhh

            def step(carry, x_t):
                h, c = carry
                g = x_t @ Wih.T + h @ Whh.T + bias
                i, f, gg, o = jnp.split(g, 4, axis=-1)
                c = jax.nn.sigmoid(f) * c + jax.nn.sigmoid(i) * jnp.tanh(gg)
                h = jax.nn.sigmoid(o) * jnp.tanh(c)
                return ((h, c), None)
            init = (jnp.zeros((N, Hd), xs.dtype), jnp.zeros((N, Hd), xs.dtype))
            (h_last, _), _ = jax.lax.scan(step, init, jnp.swapaxes(xs, 0, 1))
            return h_last
        h = jax.nn.relu(jnp.einsum('ts,bsh->bth', adj, x @ Wg0 + bg0))
        h = jax.nn.relu(jnp.einsum('ts,bsh->bth', adj, h @ Wg1 + bg1))
        Bv, Tv, Hd = h.shape
        for p in range(1, MAX_SKIP + 1):
            nw = Tv // p
            wins = h[:, :nw * p, :].reshape(Bv * nw, p, Hd)
            last = _lstm_last(Wih[p - 1], Whh[p - 1], bih[p - 1], bhh[p - 1], wins)
            idx = jnp.arange(nw) * p + (p - 1)
            h = h.at[:, idx, :].set(last.reshape(Bv, nw, Hd))
        return h

    def _L2_gnn_ref(x, adj, w1_loop, w1_neigh, b1, w2_loop, w2_neigh, b2):
        import jax, jax.numpy as jnp
        import numpy as np
        N = 3445
        B = 32
        IN_DIM = 128
        HID_DIM = 128

        def _make_adj(key):
            a = jax.random.uniform(key, (N, N), dtype=jnp.float32)
            a = (a < 0.001).astype(jnp.float32)
            a = jnp.maximum(a, a.T)
            deg = jnp.sum(a, axis=1, keepdims=True)
            return a / jnp.maximum(deg, 1.0)

        def _graph_conv(x, adj, w_loop, w_neigh, b):
            loop = jnp.einsum('bnd,dh->bnh', x, w_loop)
            neigh = jnp.einsum('nm,bmh->bnh', adj, jnp.einsum('bnd,dh->bnh', x, w_neigh))
            return loop + neigh + b
        h = jax.nn.relu(_graph_conv(x, adj, w1_loop, w1_neigh, b1))
        h = jax.nn.relu(_graph_conv(h, adj, w2_loop, w2_neigh, b2))
        return (x + h) * 0.5

    def _L3_gnn_ref(x, adj_mask, Wqkv, Wo):
        import jax, jax.numpy as jnp
        import numpy as np
        NEG = -1e+30
        B, T, C = x.shape
        qkv = x @ Wqkv
        q, k, v = jnp.split(qkv, 3, axis=-1)
        scale = 1.0 / jnp.sqrt(jnp.asarray(C, dtype=x.dtype))
        scores = jnp.einsum('btd,bsd->bts', q, k) * scale + adj_mask
        causal = jnp.tril(jnp.ones((T, T), dtype=bool))
        scores = jnp.where(causal, scores, NEG)
        attn = jax.nn.softmax(scores, axis=-1)
        y = jnp.einsum('bts,bsd->btd', attn, v)
        return y @ Wo
    x = _layernorm(x + _L0_gnn_ref(x, L0_gnn_W_lin, L0_gnn_W_val, L0_gnn_a, L0_gnn_W_out, adj, L0_gnn_src, L0_gnn_dst), axis=-1)
    x = _layernorm(x + _L1_gnn_ref(x, adj, L1_gnn_Wg0, L1_gnn_bg0, L1_gnn_Wg1, L1_gnn_bg1, L1_gnn_Wih, L1_gnn_Whh, L1_gnn_bih, L1_gnn_bhh), axis=-1)
    x = _layernorm(x + _L2_gnn_ref(x, adj, L2_gnn_w1_loop, L2_gnn_w1_neigh, L2_gnn_b1, L2_gnn_w2_loop, L2_gnn_w2_neigh, L2_gnn_b2), axis=-1)
    x = _layernorm(x + _L3_gnn_ref(x, adj, L3_gnn_Wqkv, L3_gnn_Wo), axis=-1)
    return x

_drawn_inputs = setup_inputs


def setup_inputs(seed=0):
    import zlib

    import numpy as np

    out = dict(_drawn_inputs(seed))
    spreads = {'L1_gnn_bg0': (0.0, 0.1),
     'L1_gnn_bg1': (0.0, 0.1),
     'L2_gnn_b1': (0.0, 0.268),
     'L2_gnn_b2': (0.0, 2.0)}
    factors = {'L1_gnn_Whh': 3.25}
    for name, (base, spread) in spreads.items():
        noise = np.random.default_rng([zlib.crc32(name.encode()), seed]).standard_normal(out[name].shape)
        drawn = base * np.exp(spread * noise) if base else spread * noise
        out[name] = jnp.asarray(drawn.astype(out[name].dtype))
    for name, factor in factors.items():
        out[name] = (out[name] * factor).astype(out[name].dtype)
    return out
```

```python
from contextlib import ExitStack

import concourse.bass as bass
from concourse import mybir

F32 = mybir.dt.float32
I32 = mybir.dt.int32
ALU = mybir.AluOpType
ACT = mybir.ActivationFunctionType
AX_X = mybir.AxisListType.X

P = 128
GRP = 4
BANK = GRP * P
LRELU_SLOPE = 0.2
LOG_EPS = 1e-8
LN_EPS = 1e-5
NEG = -1e30
RESET = 3e38
GATE_I, GATE_F, GATE_G, GATE_O = range(4)


def build(nc, x, adj, W_lin, W_val, a_att, W_out, src, dst, Wg0, bg0, Wg1, bg1, Wih, Whh, bih, bhh,
          w1_loop, w1_neigh, b1, w2_loop, w2_neigh, b2, Wqkv, Wo, out):
    B, N, D = x.shape
    HEADS, DH = a_att.shape
    E = src.shape[0]
    SKIPS = Wih.shape[0]
    NG = B // GRP
    EC = E // P
    BH = B * HEADS
    RT = BH // P
    GH = GRP * HEADS
    assert N == P and D == P and E == EC * P and BH == RT * P and EC * BH == BANK and SKIPS == 4
    SCALE = float(D) ** -0.5

    ctx = ExitStack()
    with ctx:
        def sb(name, shape, dt=F32):
            return ctx.enter_context(nc.sbuf_tensor(name, shape, dt))

        def sem(name):
            return ctx.enter_context(nc.semaphore(name))

        ps = ctx.enter_context(nc.psum_tensor("ps", [P, 8, BANK], F32))

        state = sb("state", [P, B, P])
        x1T_all = sb("x1T_all", [P, B, P])
        v_all = sb("v_all", [P, B, P])
        stage = sb("stage", [P, 20, BANK])

        ident = sb("ident", [P, P])
        ones = sb("ones", [P, P])
        eps_col = sb("eps_col", [P, 1])
        mhalf = sb("mhalf", [P, GRP])
        adj_sb = sb("adj_sb", [P, P])
        mask = sb("mask", [P, P])
        w_nat = sb("w_nat", [P, 3, P])
        wT = sb("wT", [P, 4, P])
        WoutT, adjT = wT[:, 2, :], wT[:, 3, :]
        wg = sb("wg", [P, 2, P])
        bg = sb("bg", [P, 2, P])
        w2 = sb("w2", [P, 4, P])
        b1_col = sb("b1_col", [P, 1])
        b2_row = sb("b2_row", [P, P])
        w3 = sb("w3", [P, 4, P])
        lstm_nat = stage[:, 0:2 * SKIPS, :].rearrange("p (w s) (g h) -> p w s g h", w=2, g=4)
        lstmT = sb("lstmT", [P, 2, SKIPS, 4, P])
        lbias_nat = sb("lbias_nat", [4 * SKIPS, 2, P])
        lbias_sum = sb("lbias_sum", [4 * SKIPS, P])
        lbias = sb("lbias", [P, 4 * SKIPS])
        a_col = sb("a_col", [P, 1])
        head_of = sb("head_of", [P, HEADS])
        a_heads = sb("a_heads", [P, HEADS])

        idx_row_i = sb("idx_row_i", [P, 2, E], I32)
        idx_col_i = sb("idx_col_i", [P, 2, EC], I32)
        idx_row = sb("idx_row", [P, 2, E])
        idx_col = sb("idx_col", [P, 2, EC])
        e_row = sb("e_row", [P, E])
        e_col = sb("e_col", [P, EC])
        key_row = sb("key_row", [P, E])
        key_col = sb("key_col", [P, EC])
        rank = sb("rank", [P, EC])
        perm = sb("perm", [P, EC, E])
        idx_wide = sb("idx_wide", [P, 2, EC, P])
        sorted_row = sb("sorted_row", [P, 2, E])
        srcT = sb("srcT", [P, E])
        dstT = sb("dstT", [P, E])
        endsT = sb("endsT", [P, E])
        src_oh = sb("src_oh", [P, EC, P])
        same = sb("same", [P, E + 1])
        reset = sb("reset", [P, E + 1])
        last = sb("last", [P, E])
        adj_pick = sb("adj_pick", [P, E])
        log_adj = sb("log_adj", [P, E])
        attT = sb("attT", [P, EC, BH])

        stats = sb("stats", [P, 3, 2, GRP, 6])
        moments = sb("moments", [P, 3, 2, GRP, 2])
        var_eps = sb("var_eps", [P, 3, 2, GRP])
        rstd = sb("rstd", [P, 3, 2, GRP])
        nmax = sb("nmax", [P, B])
        rowsum = sb("rowsum", [P, B])
        rinv = sb("rinv", [P, B])

        s_idx, s_early, s_w, s_lw, s_x = [sem(n) for n in "s_idx s_early s_w s_lw s_x".split()]
        s_pool = sem("s_pool")
        s_dve = sem("s_dve")
        s_pe0 = sem("s_pe0")
        s_act0 = sem("s_act0")
        a_xs, a_t, a_xt, a_qv, a_q, a_v, a_g, a_z, a_l, a_e = [
            sem(n) for n in "a_xs a_t a_xt a_qv a_q a_v a_g a_z a_l a_e".split()]
        c_vd, c_wv, c_y, c_ys, c_o, c_r, c_mv, c_ve, c_rs, c_xn, c_tx, c_xt, c_keep = [
            sem(n) for n in "c_vd c_wv c_y c_ys c_o c_r c_mv c_ve c_rs c_xn c_tx c_xt c_keep".split()]
        c_xw, c_xws, c_h, c_hs, c_xw2, c_xw2s, c_h2, c_h2s = [
            sem(n) for n in "c_xw c_xws c_h c_hs c_xw2 c_xw2s c_h2 c_h2s".split()]
        l_gate = [sem(f"l_gate{g}") for g in range(4)]
        l_in, l_o, l_ig, l_fc, l_c, l_tc, l_h = [
            sem(n) for n in "l_in l_o l_ig l_fc l_c l_tc l_h".split()]
        names = ("d_s d_ts d_mv1 d_ve1 d_rs1 d_x2 d_keep2 d_tx d_xt d_n1 d_n1s d_b d_h1 d_n2 d_n2s "
                 "d_d d_r1 d_r2 d_r3 d_mv2 d_ve2 d_rs2 d_x3 d_keep3 d_tx3 d_xt3 d_q d_k d_v d_qs d_ks d_vs "
                 "d_sc d_z d_mx d_p d_tp d_pt d_y d_ys d_zz d_ri d_r4 d_mv3 d_ve3 d_rs3 d_o")
        dsem = {n: sem(n) for n in names.split()}
        (d_s, d_ts, d_mv1, d_ve1, d_rs1, d_x2, d_keep2, d_tx, d_xt, d_n1, d_n1s, d_b, d_h1, d_n2, d_n2s,
         d_d, d_r1, d_r2, d_r3, d_mv2, d_ve2, d_rs2, d_x3, d_keep3, d_tx3, d_xt3, d_q, d_k, d_v, d_qs, d_ks,
         d_vs, d_sc, d_z, d_mx, d_p, d_tp, d_pt, d_y, d_ys, d_zz, d_ri, d_r4, d_mv3, d_ve3, d_rs3,
         d_o) = [dsem[n] for n in names.split()]
        d_out = [sem("d_out0"), sem("d_out1")]

        def until(eng, s, n):
            if not isinstance(n, int) or n > 0:
                eng.wait_ge(s, n)

        def run_groups(eng, step, depth):
            head = depth + 2 + depth % 2
            for t in range(head):
                step(t, t % 2)
            with eng.Fori(head, NG - 1, 2) as t:
                step(t, 0)
                step(t + 1, 1)
            for t in range(NG, NG + depth):
                step(t, t % 2)

        def active(t, offset):
            return not isinstance(t, int) or 0 <= t - offset < NG

        def grp(tile, g):
            return tile[:, bass.ds(g * GRP, GRP), :]

        def by_batch(ap):
            return ap.rearrange("p (b n) -> p b n", b=GRP)

        def per_batch_row(ap):
            return ap.rearrange("p (o n) -> p o n", o=1).broadcast_to([P, GRP, P])

        def two(first, tile=stage, n=1):
            flat = tile[:, :, :]
            return [flat[:, first + k * n:first + (k + 1) * n, :].rearrange("p s n -> p (s n)") for k in range(2)]

        v_slots = v_all[:, :, :].rearrange("p (s b) n -> p s (b n)", b=GRP)

        xs, xT, q_s = two(0), two(2), two(4)
        z_s, l_s = two(6, n=2), two(10, n=2)
        wv = two(0, n=2)
        y_s, r_s, xn, x1T, xw_s, h1_s, xw2_s = two(4), two(6), two(8), two(10), two(12), two(14), two(16)
        gate_s = [[stage[:, 4 * c + g, :] for g in range(4)] for c in range(2)]
        cell, tanh_c, hid = [[stage[:, k + c, :] for c in range(2)] for k in (8, 10, 12)]
        sum_s, x2_s, x2T, n1_s, h1T, n2_s, u_s, x3_s, x3T, v_s = [two(2 * k) for k in range(10)]
        q3, k3, z3, p3, pT, y3, o_s, t_s = [two(2 * k, v_slots) for k in range(8)]

        e_s = stage[:, 16, :]
        logit = stage[:, 17, :].rearrange("p (r e) -> p r e", r=RT)
        fmax = stage[:, 18, :].rearrange("p (r e) -> p r e", r=RT)
        bmax = stage[:, 19, :].rearrange("p (r e) -> p r e", r=RT)

        CHUNK = {1: GRP, 2: 2 * GRP, 3: 2 * GRP, 4: 4 * GRP}
        PAIRS = {p: B // CHUNK[p] // 2 for p in CHUNK}
        UNIT0 = {p: sum(PAIRS[q] * 2 * q for q in range(1, p)) for p in range(1, SKIPS + 2)}
        FGATE0 = {p: sum(PAIRS[q] * 2 * (q - 1) for q in range(1, p)) for p in range(1, SKIPS + 2)}
        UNITS_ALL = UNIT0[SKIPS] + PAIRS[SKIPS] * 2 * SKIPS

        def wins(p):
            return N // p

        def cols(p):
            return CHUNK[p] * wins(p)

        def at_step(p, i, c, s):
            w = wins(p)
            return state[:, bass.ds((2 * i + c) * CHUNK[p], CHUNK[p]), s:s + (w - 1) * p + 1:p]

        def windows(ap, p):
            return ap[:, 0:cols(p)].rearrange("q (b w) -> q b w", b=CHUNK[p])

        def unit(p, i, s, c):
            return UNIT0[p] + 2 * p * i + 2 * s + c

        def fgate(p, i, s, c):
            return FGATE0[p] + 2 * (p - 1) * i + 2 * (s - 1) + c

        def run_pairs(eng, pair):
            for p in range(1, SKIPS + 1):
                if p == 1:
                    pair(p, 0)
                with eng.Fori(1 if p == 1 else 0, PAIRS[p]) as i:
                    pair(p, i)

        block = ctx.enter_context(nc.Block())

        (PE_WT, PE_SORTED, PE_PICK, PE_ADJ, PE_BIAS, PE_LOGIT) = range(1, 7)
        PE_LSTM = [PE_LOGIT + 1 + k for k in range(2 * SKIPS)]
        PE_ATT = PE_LSTM[-1] + 1
        (ACT_WT, ACT_LOG, ACT_SRC) = range(1, 4)
        ACT_LSTM = ACT_SRC + 2 * SKIPS
        ACT_EXP = ACT_LSTM + 1
        POOL_CONST = 7
        DV_PERM = 4 + 4 * EC
        DV_ONEHOT = DV_PERM + 4
        DV_PICK = DV_ONEHOT + 4
        DV_BIAS = DV_PICK + 1
        DV_LOGIT = DV_BIAS + 3
        DV_DIFF = DV_LOGIT + 2 * RT + 2
        DV_ATT = DV_DIFF + 3 * RT + 2
        DV_ATTT = DV_ATT + 1

        @block.sync
        def _(sp):
            as_row = lambda v: v.rearrange("(o n) -> o n", o=1)
            for k, v in enumerate((src, dst)):
                sp.dma_start(idx_row_i[:, k, :], as_row(v).broadcast_to([P, E])).then_inc(s_idx, 16)
                sp.dma_start(idx_col_i[:, k, :], v.rearrange("(c p) -> p c", c=EC),
                             allow_slow_non_contiguous=True).then_inc(s_idx, 16)
            sp.dma_start(adj_sb[:], adj).then_inc(s_early, 16)
            for k, w in enumerate((W_lin, W_val, W_out)):
                sp.dma_start(w_nat[:, k, :], w).then_inc(s_early, 16)
            sp.dma_start(a_col[:], a_att.rearrange("h (d o) -> (h d) o", o=1),
                         allow_slow_non_contiguous=True).then_inc(s_early, 16)
            xr = x.rearrange("b n d -> n b d")
            for k in range(4):
                sp.dma_start(state[:, k * B // 4:(k + 1) * B // 4, :],
                             xr[:, k * B // 4:(k + 1) * B // 4, :]).then_inc(s_x, 16)
            for k, (w, b) in enumerate(((Wg0, bg0), (Wg1, bg1))):
                sp.dma_start(wg[:, k, :], w).then_inc(s_w, 16)
                sp.dma_start(bg[:, k, :], as_row(b).broadcast_to([P, P])).then_inc(s_w, 16)
            for k, w in enumerate((w1_loop, w1_neigh, w2_loop, w2_neigh)):
                sp.dma_start(w2[:, k, :], w).then_inc(s_w, 16)
            sp.dma_start(w3[:, 0:3, :], Wqkv.rearrange("c (k n) -> c k n", k=3)).then_inc(s_w, 16)
            sp.dma_start(w3[:, 3, :], Wo).then_inc(s_w, 16)
            sp.dma_start(b1_col[:], b1.rearrange("(p o) -> p o", o=1),
                         allow_slow_non_contiguous=True).then_inc(s_w, 16)
            sp.dma_start(b2_row[:], as_row(b2).broadcast_to([P, P])).then_inc(s_w, 16)
            for k, b in enumerate((bih, bhh)):
                sp.dma_start(lbias_nat[:, k, :], b.rearrange("p (g r) -> (p g) r", g=4)).then_inc(s_w, 16)
            sp.wait_ge(a_e, NG)
            for k, w in enumerate((Wih, Whh)):
                for p in range(SKIPS):
                    sp.dma_start(lstm_nat[:, k, p], w[p].rearrange("(g r) h -> r g h", g=4)).then_inc(s_lw, 16)

            def step(t, u):
                if active(t, 4):
                    g, k = t - 4, (u - 4) % 2
                    sp.wait_ge(d_o, g + 1)
                    sp.dma_start(out[bass.ds(g * GRP, GRP)].rearrange("b n d -> n b d"),
                                 by_batch(o_s[k])).then_inc(d_out[k], 16)
            run_groups(sp, step, 4)
            for k in range(2):
                sp.wait_ge(d_out[k], 16 * NG // 2)

        @block.gpsimd
        def _(pool):
            nc.gpsimd.iota(e_row[:], pattern=[[1, E]], base=0, channel_multiplier=0,
                           allow_small_or_imprecise_dtypes=True)
            nc.gpsimd.iota(e_col[:], pattern=[[P, EC]], base=0, channel_multiplier=1,
                           allow_small_or_imprecise_dtypes=True).then_inc(s_pool, 1)
            nc.gpsimd.memset(ones[:], 1.0)
            nc.gpsimd.memset(mhalf[:], -0.5)
            nc.gpsimd.memset(head_of[:], 1.0)
            nc.gpsimd.memset(eps_col[:], LOG_EPS)
            nc.gpsimd.memset(ident[:], 0.0).then_inc(s_pool, 1)
            pool.wait_ge(s_pool, 2)
            nc.gpsimd.affine_select(out=ident[:], in_=ident[:], compare_op=ALU.not_equal, fill=1.0, base=0,
                                    pattern=[[-1, P]], channel_multiplier=1).then_inc(s_pool, 1)
            nc.gpsimd.affine_select(out=head_of[:], in_=head_of[:], compare_op=ALU.is_ge, fill=0.0, base=0,
                                    pattern=[[-DH, HEADS]], channel_multiplier=1).then_inc(s_pool, 1)
            pool.wait_ge(s_pool, 4)
            nc.gpsimd.affine_select(out=head_of[:], in_=head_of[:], compare_op=ALU.is_ge, fill=0.0, base=DH - 1,
                                    pattern=[[DH, HEADS]], channel_multiplier=-1).then_inc(s_pool, 1)
            pool.wait_ge(s_early, 5 * 16)
            nc.gpsimd.affine_select(out=mask[:], in_=adj_sb[:], compare_op=ALU.is_ge, fill=NEG, base=0,
                                    pattern=[[-1, P]], channel_multiplier=1).then_inc(s_pool, 1)
            nc.gpsimd.memset(same[:], 0.0).then_inc(s_pool, 1)

            pool.wait_ge(s_x, 4 * 16)

            def step_a(t, u):
                if active(t, 0):
                    until(pool, a_t, t - 1)
                    nc.gpsimd.tensor_copy(by_batch(xs[u]), grp(state, t)).then_inc(a_xs, 1)
            run_groups(pool, step_a, 3)

            def rstd_of(k, n, buf, s_ve, s_rs):
                pool.wait_ge(s_ve, n)
                nc.gpsimd.tensor_tensor(rstd[:, k, buf, :], var_eps[:, k, buf, :], mhalf[:], ALU.pow).then_inc(s_rs, 1)

            def step_c(t, u):
                if active(t, 2):
                    g, k = t - 2, u
                    pool.wait_ge(c_xt, g + 1)
                    nc.gpsimd.tensor_copy(grp(x1T_all, g), by_batch(x1T[k])).then_inc(c_keep, 1)
                if active(t, 1):
                    rstd_of(0, t, (u - 1) % 2, c_ve, c_rs)
            run_groups(pool, step_c, 3)

            pool.wait_ge(l_h, UNITS_ALL)

            def step_d(t, u):
                if active(t, 0):
                    until(pool, d_ts, t - 1)
                    nc.gpsimd.tensor_tensor(by_batch(sum_s[u]), grp(x1T_all, t), grp(state, t),
                                            ALU.add).then_inc(d_s, 1)
                if active(t, 2):
                    rstd_of(1, t - 1, u, d_ve2, d_rs2)
                if active(t, 0):
                    rstd_of(0, t + 1, u, d_ve1, d_rs1)
                if active(t, 2):
                    g = t - 2
                    pool.wait_ge(d_x3, g + 1)
                    nc.gpsimd.tensor_copy(grp(state, g), by_batch(x3_s[u])).then_inc(d_keep3, 1)
                if active(t, 0):
                    pool.wait_ge(d_x2, t + 1)
                if active(t, 4):
                    rstd_of(2, t - 3, u, d_ve3, d_rs3)
                if active(t, 0):
                    nc.gpsimd.tensor_copy(grp(state, t), by_batch(x2_s[u])).then_inc(d_keep2, 1)
            run_groups(pool, step_d, 4)

        @block.tensor
        def _(pe):
            mm = nc.tensor.matmul

            pe.wait_ge(s_pool, 3)
            pe.wait_ge(s_early, 5 * 16)
            for k in range(3):
                nc.tensor.transpose(ps[:, 0, k * P:(k + 1) * P], w_nat[:, k, :], ident[:])
            nc.tensor.transpose(ps[:, 0, 3 * P:4 * P], adj_sb[:], ident[:]).then_inc(s_pe0, 1)
            pe.wait_ge(s_dve, DV_PERM)
            for k in range(2):
                for c in range(EC):
                    m = mm(ps[:, 6, k * E:(k + 1) * E], idx_wide[:, k, c, :], perm[:, c, :],
                           start=c == 0, stop=c == EC - 1)
            m.then_inc(s_pe0, 1)
            pe.wait_ge(s_dve, DV_ONEHOT)
            mm(ps[:, 7, 0:E], adj_sb[:], srcT[:], start=True, stop=True)
            for c in range(EC):
                m = nc.tensor.transpose(ps[:, 5, c * P:(c + 1) * P], srcT[:, c * P:(c + 1) * P], ident[:])
            m.then_inc(s_pe0, 1)
            pe.wait_ge(s_dve, DV_PICK)
            mm(ps[:, 6, 0:E], ones[:], adj_pick[:], start=True, stop=True).then_inc(s_pe0, 1)
            pe.wait_ge(s_dve, DV_BIAS)
            nc.tensor.transpose(ps[:, 7, 0:4 * SKIPS], lbias_sum[:], ident[0:4 * SKIPS, 0:4 * SKIPS])\
                .then_inc(s_pe0, 1)

            pe.wait_ge(s_act0, ACT_SRC)

            def step_a(t, u):
                if active(t, 1):
                    g, k = t - 1, (u - 1) % 2
                    pe.wait_ge(a_xt, g + 1)
                    until(pe, a_q, g)
                    until(pe, a_v, g)
                    qv = ps[:, 1:3, :].rearrange("p s n -> p (s n)")
                    for b in range(GRP):
                        m = mm(qv[:, b * 2 * P:(b + 1) * 2 * P], xT[k][:, b * P:(b + 1) * P],
                               wT[:, 0:2, :].rearrange("p k n -> p (k n)"), start=True, stop=True)
                    m.then_inc(a_qv, 1)
                if active(t, 3):
                    g, k = t - 3, (u - 3) % 2
                    pe.wait_ge(a_l, g + 1)
                    for b in range(GRP):
                        for c in range(EC):
                            at = (b * EC + c) * P
                            m = mm(ps[:, 5, bass.ds(c * BH + (g * GRP + b) * HEADS, HEADS)],
                                   l_s[k][:, at:at + P], a_heads[:], start=True, stop=True)
                    m.then_inc(a_e, 1)
                if active(t, 0):
                    pe.wait_ge(a_xs, t + 1)
                    until(pe, a_xt, t)
                    for b in range(GRP):
                        m = nc.tensor.transpose(ps[:, 0, b * P:(b + 1) * P], xs[u][:, b * P:(b + 1) * P], ident[:])
                    m.then_inc(a_t, 1)
                if active(t, 2):
                    g, k = t - 2, u
                    pe.wait_ge(a_q, g + 1)
                    until(pe, a_l, g)
                    gs = ps[:, 3:5, :].rearrange("p s n -> p (s n)")
                    for b in range(GRP):
                        m = mm(gs[:, b * E:(b + 1) * E], q_s[k][:, b * P:(b + 1) * P], endsT[:],
                               start=True, stop=True)
                    m.then_inc(a_g, 1)
            run_groups(pe, step_a, 3)

            pe.wait_ge(s_dve, DV_LOGIT)
            for r in range(RT):
                for c in range(EC):
                    m = nc.tensor.transpose(ps[:, 0, r * E + c * P:r * E + (c + 1) * P],
                                            e_s[:, c * BH + r * P:c * BH + (r + 1) * P], ident[:])
            m.then_inc(s_pe0, 1)
            pe.wait_ge(s_lw, 2 * SKIPS * 16)
            for n in range(2 * SKIPS):
                if n >= 2:
                    pe.wait_ge(s_act0, ACT_SRC + n - 1)
                for q in range(4):
                    m = nc.tensor.transpose(ps[:, 1 + n % 2, q * P:(q + 1) * P],
                                            lstm_nat[:, n // SKIPS, n % SKIPS, q, :], ident[:])
                m.then_inc(s_pe0, 1)
            pe.wait_ge(s_dve, DV_ATT)
            for r in range(RT):
                for c in range(EC):
                    m = nc.tensor.transpose(ps[:, 3, c * BH + r * P:c * BH + (r + 1) * P],
                                            logit[:, r, c * P:(c + 1) * P], ident[:])
            m.then_inc(s_pe0, 1)

            pe.wait_ge(s_act0, ACT_EXP)
            pe.wait_ge(s_dve, DV_ATTT)
            pe.wait_ge(s_w, 14 * 16)

            def project(bank, src_s, w, sem_):
                for b in range(GRP):
                    m = mm(ps[:, bank, b * P:(b + 1) * P], src_s[:, b * P:(b + 1) * P], w, start=True, stop=True)
                m.then_inc(sem_, 1)

            def step_c(t, u):
                if active(t, 1):
                    g, k = t - 1, (u - 1) % 2
                    pe.wait_ge(c_wv, g + 1)
                    until(pe, c_ys, g)
                    for b in range(GRP):
                        for c in range(EC):
                            m = mm(ps[:, 2, b * P:(b + 1) * P], wv[k][:, c * BANK + b * P:c * BANK + (b + 1) * P],
                                   src_oh[:, c, :], start=c == 0, stop=c == EC - 1)
                    m.then_inc(c_y, 1)
                if active(t, 2):
                    g, k = t - 2, u
                    pe.wait_ge(c_xn, g + 1)
                    until(pe, c_hs, g)
                    for b in range(GRP):
                        m = nc.tensor.transpose(ps[:, 3, b * P:(b + 1) * P], xn[k][:, b * P:(b + 1) * P], ident[:])
                    m.then_inc(c_tx, 1)
                if active(t, 3):
                    g, k = t - 3, (u - 3) % 2
                    pe.wait_ge(c_hs, g + 1)
                    until(pe, c_xw2s, g)
                    project(4, h1_s[k], wg[:, 1, :], c_xw2)
                if active(t, 1):
                    g, k = t - 1, (u - 1) % 2
                    pe.wait_ge(c_ys, g + 1)
                    until(pe, c_r, g)
                    project(5, y_s[k], WoutT, c_o)
                if active(t, 2):
                    g, k = t - 2, u
                    pe.wait_ge(c_xt, g + 1)
                    until(pe, c_xws, g)
                    project(6, x1T[k], wg[:, 0, :], c_xw)
                if active(t, 0):
                    until(pe, c_wv, t)
                    for c in range(EC):
                        m = mm(ps[:, c, :], dstT[:, c * P:(c + 1) * P], grp(v_all, t), start=True, stop=True)
                    m.then_inc(c_vd, 1)
                if active(t, 3):
                    g, k = t - 3, (u - 3) % 2
                    pe.wait_ge(c_xw2s, g + 1)
                    until(pe, c_h2s, g)
                    project(7, xw2_s[k], adjT, c_h2)
                if active(t, 2):
                    g, k = t - 2, u
                    pe.wait_ge(c_xws, g + 1)
                    project(3, xw_s[k], adjT, c_h)
            run_groups(pe, step_c, 3)

            pe.wait_ge(c_h2s, NG)

            def pair(p, i):
                for s in range(p):
                    gates = (GATE_I, GATE_G, GATE_O) if s == 0 else (GATE_F, GATE_I, GATE_G, GATE_O)
                    for c in range(2):
                        n = unit(p, i, s, c)
                        until(pe, l_o, n - 1)
                        if s == 0 and p == 2:
                            pe.wait_ge(l_h, UNIT0[1] + 4 * i + 2 * c + 2)
                        if s == 0 and p == 3:
                            pe.wait_ge(l_h, UNIT0[2] + 4 * i + 2 + c + 1)
                        if s == 0 and p == 4:
                            pe.wait_ge(l_h, UNIT0[3] + 12 * i + 6 * c + 6)
                        for q in gates:
                            m = mm(windows(ps[:, 4 * c + q, :], p), lstmT[:, 0, p - 1, q, :], at_step(p, i, c, s),
                                   start=True, stop=s == 0)
                            if s == 0:
                                m.then_inc(l_gate[q], 1)
                        if s > 0:
                            pe.wait_ge(l_h, n - 1)
                            for q in gates:
                                mm(ps[:, 4 * c + q, 0:cols(p)], lstmT[:, 1, p - 1, q, :], hid[c][:, 0:cols(p)],
                                   start=False, stop=True).then_inc(l_gate[q], 1)
            run_pairs(pe, pair)

            pe.wait_ge(l_o, UNITS_ALL)

            def transposes(bank, src_s, sem_):
                for b in range(GRP):
                    m = nc.tensor.transpose(ps[:, bank, b * P:(b + 1) * P], src_s[:, b * P:(b + 1) * P], ident[:])
                m.then_inc(sem_, 1)

            def step_d(t, u):
                if active(t, 2):
                    g, k = t - 2, u
                    pe.wait_ge(d_n2s, g + 1)
                    until(pe, d_xt3, g)
                    mm(ps[:, 0, :], adjT, n2_s[k], start=True, stop=False, skip_group_check=True)
                    for b in range(GRP):
                        m = mm(ps[:, 0, b * P:(b + 1) * P], h1T[k][:, b * P:(b + 1) * P], w2[:, 2, :],
                               start=False, stop=b == GRP - 1, skip_group_check=True)
                    m.then_inc(d_d, 1)
                if active(t, 1):
                    g, k = t - 1, (u - 1) % 2
                    pe.wait_ge(d_x2, g + 1)
                    until(pe, d_h1, g)
                    transposes(1, x2_s[k], d_tx)
                if active(t, 0):
                    pe.wait_ge(d_s, t + 1)
                    until(pe, d_x2, t)
                    transposes(2, sum_s[u], d_ts)
                if active(t, 4):
                    g, k = t - 4, u
                    pe.wait_ge(d_ys, g + 1)
                    project(3, y3[k], w3[:, 3, :], d_zz)
                if active(t, 1):
                    g, k = t - 1, (u - 1) % 2
                    pe.wait_ge(d_xt, g + 1)
                    until(pe, d_ks, g - 1)
                    project(4, x2T[k], w2[:, 1, :], d_n1)
                if active(t, 3):
                    g, k = t - 3, (u - 3) % 2
                    pe.wait_ge(d_p, g + 1)
                    pe.wait_ge(d_vs, g + 1)
                    transposes(5, p3[k], d_tp)
                if active(t, 1):
                    g, k = t - 1, (u - 1) % 2
                    mm(ps[:, 1, :], w2[:, 0, :], x2T[k], start=True, stop=False, skip_group_check=True)
                    pe.wait_ge(d_n1s, g + 1)
                    for b in range(GRP):
                        m = mm(ps[:, 1, b * P:(b + 1) * P], n1_s[k][:, b * P:(b + 1) * P], adjT,
                               start=False, stop=b == GRP - 1, skip_group_check=True)
                    m.then_inc(d_b, 1)
                if active(t, 2):
                    g, k = t - 2, u
                    pe.wait_ge(d_x3, g + 1)
                    transposes(0, x3_s[k], d_tx3)
                if active(t, 3):
                    g, k = t - 3, (u - 3) % 2
                    pe.wait_ge(d_pt, g + 1)
                    until(pe, d_r4, g)
                    for b in range(GRP):
                        m = mm(ps[:, 3, b * P:(b + 1) * P], v_s[k][:, b * P:(b + 1) * P],
                               pT[k][:, b * P:(b + 1) * P], start=True, stop=True)
                    m.then_inc(d_y, 1)
                if active(t, 2):
                    g, k = t - 2, u
                    pe.wait_ge(d_xt3, g + 1)
                    until(pe, d_z, g)
                    mm(ps[:, 6, :], w3[:, 0, :], x3T[k], start=True, stop=True).then_inc(d_q, 1)
                    until(pe, d_n1s, min(t, NG) if isinstance(t, int) else t)
                    mm(ps[:, 4, :], w3[:, 1, :], x3T[k], start=True, stop=True).then_inc(d_k, 1)
                    until(pe, d_pt, g)
                    project(5, x3T[k], w3[:, 2, :], d_v)
                if active(t, 1):
                    g, k = t - 1, (u - 1) % 2
                    pe.wait_ge(d_h1, g + 1)
                    until(pe, d_n2s, g)
                    project(7, h1T[k], w2[:, 3, :], d_n2)
                if active(t, 2):
                    g, k = t - 2, u
                    pe.wait_ge(d_qs, g + 1)
                    pe.wait_ge(d_ks, g + 1)
                    for b in range(GRP):
                        m = mm(ps[:, 6, b * P:(b + 1) * P], q3[k][:, b * P:(b + 1) * P],
                               k3[k][:, b * P:(b + 1) * P], start=True, stop=True)
                    m.then_inc(d_sc, 1)
            run_groups(pe, step_d, 4)

        @block.scalar
        def _(act):
            act.wait_ge(s_pe0, PE_WT)
            nc.scalar.copy(wT[:].rearrange("p k n -> p (k n)"), ps[:, 0, :]).then_inc(s_act0, 1)
            act.wait_ge(s_pool, 2)
            act.wait_ge(s_pe0, PE_ADJ)
            nc.scalar.activation(log_adj[:], ps[:, 6, 0:E], ACT.Ln, bias=eps_col[:]).then_inc(s_act0, 1)
            act.wait_ge(s_pe0, PE_PICK)
            nc.scalar.copy(src_oh[:].rearrange("p c n -> p (c n)"), ps[:, 5, 0:EC * P]).then_inc(s_act0, 1)

            def step_a(t, u):
                if active(t, 0):
                    act.wait_ge(a_t, t + 1)
                    until(act, a_qv, t - 1)
                    nc.scalar.copy(xT[u], ps[:, 0, :]).then_inc(a_xt, 1)
                if active(t, 2):
                    g, k = t - 2, u
                    act.wait_ge(a_g, g + 1)
                    until(act, a_l, g - 1)
                    nc.scalar.copy(z_s[k], ps[:, 3:5, :].rearrange("p s n -> p (s n)")).then_inc(a_z, 1)
            run_groups(act, step_a, 3)

            for n in range(2 * SKIPS):
                act.wait_ge(s_pe0, PE_LSTM[n])
                nc.scalar.copy(lstmT[:, n // SKIPS, n % SKIPS].rearrange("p q h -> p (q h)"),
                               ps[:, 1 + n % 2, :]).then_inc(s_act0, 1)
            act.wait_ge(s_dve, DV_DIFF)
            nc.scalar.activation(fmax[:].rearrange("p r e -> p (r e)"), logit[:].rearrange("p r e -> p (r e)"),
                                 ACT.Exp).then_inc(s_act0, 1)

            def step_c(t, u):
                if active(t, 1):
                    g, k = t - 1, (u - 1) % 2
                    act.wait_ge(c_y, g + 1)
                    until(act, c_o, g - 1)
                    nc.scalar.copy(y_s[k], ps[:, 2, :]).then_inc(c_ys, 1)
                if active(t, 2):
                    g, k = t - 2, u
                    act.wait_ge(c_tx, g + 1)
                    until(act, c_xw, g - 1)
                    until(act, c_keep, g - 1)
                    nc.scalar.copy(x1T[k], ps[:, 3, :]).then_inc(c_xt, 1)
                if active(t, 3):
                    g = t - 3
                    act.wait_ge(c_h2, g + 1)
                    nc.scalar.activation(grp(state, g), by_batch(ps[:, 7, :]), ACT.Relu).then_inc(c_h2s, 1)
                if active(t, 2):
                    g, k = t - 2, u
                    act.wait_ge(c_h, g + 1)
                    until(act, c_xw2, g - 1)
                    nc.scalar.activation(h1_s[k], ps[:, 3, :], ACT.Relu).then_inc(c_hs, 1)
            run_groups(act, step_c, 3)

            def gates(p, i, s, c):
                n = unit(p, i, s, c)
                until(act, l_h, n - 1)
                for q in (GATE_I, GATE_G, GATE_O) if s == 0 else (GATE_F, GATE_I, GATE_G, GATE_O):
                    act.wait_ge(l_gate[q], fgate(p, i, s, c) + 1 if q == GATE_F else n + 1)
                    a = nc.scalar.activation(gate_s[c][q][:, 0:cols(p)], ps[:, 4 * c + q, 0:cols(p)],
                                             ACT.Tanh if q == GATE_G else ACT.Sigmoid,
                                             bias=lbias[:, 4 * (p - 1) + q:4 * (p - 1) + q + 1])
                    if q == GATE_G:
                        a.then_inc(l_in, 1)
                    if q == GATE_O:
                        a.then_inc(l_o, 1)

            def squash(p, i, s, c):
                act.wait_ge(l_c, unit(p, i, s, c) + 1)
                nc.scalar.activation(tanh_c[c][:, 0:cols(p)], cell[c][:, 0:cols(p)], ACT.Tanh).then_inc(l_tc, 1)

            def pair(p, i):
                for c in range(2):
                    gates(p, i, 0, c)
                for c in range(2):
                    squash(p, i, 0, c)
                for s in range(1, p):
                    for c in range(2):
                        gates(p, i, s, c)
                        squash(p, i, s, c)
            act.wait_ge(c_keep, NG)
            run_pairs(act, pair)

            def step_d(t, u):
                if active(t, 1):
                    g, k = t - 1, (u - 1) % 2
                    act.wait_ge(d_tx, g + 1)
                    until(act, d_b, g - 1)
                    nc.scalar.copy(x2T[k], ps[:, 1, :]).then_inc(d_xt, 1)
                    act.wait_ge(d_n1, g + 1)
                    nc.scalar.copy(n1_s[k], ps[:, 4, :]).then_inc(d_n1s, 1)
                if active(t, 3):
                    g, k = t - 3, (u - 3) % 2
                    act.wait_ge(d_tp, g + 1)
                    until(act, d_y, g - 1)
                    nc.scalar.copy(pT[k], ps[:, 5, :]).then_inc(d_pt, 1)
                if active(t, 1):
                    g, k = t - 1, (u - 1) % 2
                    act.wait_ge(d_b, g + 1)
                    until(act, d_d, g - 1)
                    nc.scalar.activation(h1T[k], ps[:, 1, :], ACT.Relu, bias=b1_col[:]).then_inc(d_h1, 1)
                if active(t, 2):
                    g, k = t - 2, u
                    act.wait_ge(d_tx3, g + 1)
                    until(act, d_v, g - 1)
                    nc.scalar.copy(x3T[k], ps[:, 0, :]).then_inc(d_xt3, 1)
                if active(t, 3):
                    g, k = t - 3, (u - 3) % 2
                    act.wait_ge(d_y, g + 1)
                    until(act, d_zz, g - 1)
                    nc.scalar.copy(y3[k], ps[:, 3, :]).then_inc(d_ys, 1)
                if active(t, 2):
                    g, k = t - 2, u
                    act.wait_ge(d_q, g + 1)
                    until(act, d_sc, g - 1)
                    nc.scalar.activation(q3[k], ps[:, 6, :], ACT.Copy, scale=SCALE).then_inc(d_qs, 1)
                    act.wait_ge(d_k, g + 1)
                    nc.scalar.copy(k3[k], ps[:, 4, :]).then_inc(d_ks, 1)
                    act.wait_ge(d_v, g + 1)
                    until(act, d_y, g - 1)
                    nc.scalar.copy(v_s[k], ps[:, 5, :]).then_inc(d_vs, 1)
                if active(t, 1):
                    g, k = t - 1, (u - 1) % 2
                    act.wait_ge(d_n2, g + 1)
                    until(act, d_d, g - 1)
                    nc.scalar.copy(n2_s[k], ps[:, 7, :]).then_inc(d_n2s, 1)
                if active(t, 2):
                    g, k = t - 2, u
                    act.wait_ge(d_mx, g + 1)
                    until(act, d_tp, g - 1)
                    for b in range(GRP):
                        at = bass.ds(g * GRP + b, 1)
                        a = nc.scalar.activation(p3[k][:, b * P:(b + 1) * P], z3[k][:, b * P:(b + 1) * P], ACT.Exp,
                                                 bias=nmax[:, at], accum_out=rowsum[:, at])
                    a.then_inc(d_p, 1)
            run_groups(act, step_d, 4)

        @block.vector
        def _(dve):
            v = nc.vector
            count = [0]

            def link(ins):
                count[0] += 1
                ins.then_inc(s_dve, 1)
                dve.wait_ge(s_dve, count[0])

            dve.wait_ge(s_idx, 4 * 16)
            dve.wait_ge(s_pool, 1)
            link(v.tensor_copy(idx_row[:].rearrange("p k e -> p (k e)"), idx_row_i[:].rearrange("p k e -> p (k e)")))
            link(v.tensor_copy(idx_col[:].rearrange("p k c -> p (k c)"), idx_col_i[:].rearrange("p k c -> p (k c)")))
            link(v.scalar_tensor_tensor(out=key_row[:], in0=idx_row[:, 0, :], scalar=float(E), in1=e_row[:],
                                        op0=ALU.mult, op1=ALU.add))
            link(v.scalar_tensor_tensor(out=key_col[:], in0=idx_col[:, 0, :], scalar=float(E), in1=e_col[:],
                                        op0=ALU.mult, op1=ALU.add))
            for c in range(EC):
                link(v.tensor_scalar(perm[:, c, :], key_row[:], key_col[:, c:c + 1], None, ALU.is_lt, ALU.add,
                                     accum_out=rank[:, c:c + 1]))
            dve.wait_ge(s_pool, 2)
            for c in range(EC):
                link(v.tensor_scalar(perm[:, c, :], e_row[:], rank[:, c:c + 1], None, ALU.is_equal))
                for k in range(2):
                    link(v.tensor_scalar(idx_wide[:, k, c, :], ones[:], idx_col[:, k, c:c + 1], None, ALU.mult))
            assert count[0] == DV_PERM
            dve.wait_ge(s_pe0, PE_SORTED)
            link(v.tensor_copy(sorted_row[:].rearrange("p k e -> p (k e)"), ps[:, 6, :]))
            link(v.tensor_scalar(srcT[:], sorted_row[:, 0, :], e_col[:, 0:1], None, ALU.is_equal))
            link(v.tensor_scalar(dstT[:], sorted_row[:, 1, :], e_col[:, 0:1], None, ALU.is_equal))
            link(v.tensor_tensor(endsT[:], srcT[:], dstT[:], ALU.add))
            assert count[0] == DV_ONEHOT
            dve.wait_ge(s_pool, POOL_CONST)
            link(v.tensor_tensor(same[:, 1:E], sorted_row[:, 0, 1:E], sorted_row[:, 0, 0:E - 1], ALU.is_equal))
            link(v.tensor_scalar(reset[:], same[:], -1.0, RESET, ALU.add, ALU.mult))
            link(v.tensor_scalar(last[:], same[:, 1:E + 1], -1.0, 1.0, ALU.mult, ALU.add))
            dve.wait_ge(s_pe0, PE_PICK)
            link(v.tensor_tensor(adj_pick[:], ps[:, 7, 0:E], dstT[:], ALU.mult))
            assert count[0] == DV_PICK
            dve.wait_ge(s_w, 14 * 16)
            link(v.tensor_tensor(lbias_sum[:], lbias_nat[:, 0, :], lbias_nat[:, 1, :], ALU.add))
            assert count[0] == DV_BIAS
            link(v.tensor_scalar(a_heads[:], head_of[:], a_col[:], None, ALU.mult))
            dve.wait_ge(s_pe0, PE_BIAS)
            link(v.tensor_copy(lbias[:], ps[:, 7, 0:4 * SKIPS]))

            def step_a(t, u):
                if active(t, 2):
                    g, k = t - 2, u
                    dve.wait_ge(a_z, g + 1)
                    until(dve, a_e, g - 1)
                    v.scalar_tensor_tensor(out=l_s[k], in0=z_s[k], scalar=LRELU_SLOPE, in1=z_s[k],
                                           op0=ALU.mult, op1=ALU.max).then_inc(a_l, 1)
                if active(t, 1):
                    g, k = t - 1, (u - 1) % 2
                    dve.wait_ge(a_qv, g + 1)
                    until(dve, a_g, g - 1)
                    qv = ps[:, 1:3, :].rearrange("p s (b w n) -> p (s b) w n", b=GRP // 2, w=2)
                    v.tensor_copy(by_batch(q_s[k]), qv[:, :, 0, :]).then_inc(a_q, 1)
                    v.tensor_copy(grp(v_all, g), qv[:, :, 1, :]).then_inc(a_v, 1)
            run_groups(dve, step_a, 3)

            dve.wait_ge(a_e, NG)
            link(v.tensor_copy(e_s, ps[:, 5, :]))
            assert count[0] == DV_LOGIT
            dve.wait_ge(s_pe0, PE_LOGIT)
            dve.wait_ge(s_act0, ACT_LOG)
            link(v.tensor_tensor(logit, ps[:, 0, :].rearrange("p (r e) -> p r e", r=RT),
                                 log_adj[:].rearrange("p (o e) -> p o e", o=1).broadcast_to([P, RT, E]), ALU.add))
            for r in range(RT):
                link(v.tensor_tensor_scan(fmax[:, r, :], reset[:, 0:E], logit[:, r, :], 0.0, ALU.add, ALU.max))
                link(v.tensor_tensor_scan(bmax[:, r, ::-1], reset[:, 1:E + 1][:, ::-1], fmax[:, r, ::-1], 0.0,
                                          ALU.add, ALU.max))
            link(v.tensor_tensor(logit, logit, bmax, ALU.subtract))
            assert count[0] == DV_DIFF
            dve.wait_ge(s_act0, ACT_EXP)
            for r in range(RT):
                link(v.tensor_tensor_scan(bmax[:, r, :], same[:, 0:E], fmax[:, r, :], 0.0, ALU.mult, ALU.add))
                link(v.tensor_tensor(bmax[:, r, :], bmax[:, r, :], last[:], ALU.mult))
                link(v.tensor_tensor_scan(logit[:, r, ::-1], same[:, 1:E + 1][:, ::-1], bmax[:, r, ::-1], 0.0,
                                          ALU.mult, ALU.add))
            link(v.reciprocal(bmax, logit))
            link(v.tensor_tensor(logit, fmax, bmax, ALU.mult))
            assert count[0] == DV_ATT
            dve.wait_ge(s_pe0, PE_ATT)
            link(v.tensor_copy(attT[:].rearrange("p c n -> p (c n)"), ps[:, 3, :]))
            assert count[0] == DV_ATTT

            def ln_moments(j, src_b, buf, n, s_mv, s_ve):
                for b in range(GRP):
                    v.bn_stats(stats[:, j, buf, b, :], src_b[:, b * P:(b + 1) * P])
                dve.drain()
                for b in range(GRP):
                    m = v.bn_aggr(moments[:, j, buf, b, :], stats[:, j, buf, b, :])
                m.then_inc(s_mv, 1)
                dve.wait_ge(s_mv, n)
                v.tensor_scalar(var_eps[:, j, buf, :], moments[:, j, buf, :, 1], LN_EPS, None,
                                ALU.add).then_inc(s_ve, 1)

            def ln_scale(j, dst_b, src_b, buf, n, s_rs, s_out):
                dve.wait_ge(s_rs, n)
                for b in range(GRP):
                    m = v.tensor_scalar(dst_b[:, b * P:(b + 1) * P], src_b[:, b * P:(b + 1) * P],
                                        moments[:, j, buf, b, 0:1], rstd[:, j, buf, b:b + 1],
                                        ALU.subtract, ALU.mult)
                m.then_inc(s_out, 1)

            def step_c(t, u):
                if active(t, 3):
                    g, k = t - 3, (u - 3) % 2
                    dve.wait_ge(c_xw2, g + 1)
                    until(dve, c_h2, g - 1)
                    v.tensor_tensor(by_batch(xw2_s[k]), by_batch(ps[:, 4, :]), per_batch_row(bg[:, 1, :]),
                                    ALU.add).then_inc(c_xw2s, 1)
                if active(t, 1):
                    g, k = t - 1, (u - 1) % 2
                    dve.wait_ge(c_o, g + 1)
                    v.tensor_tensor(by_batch(r_s[k]), by_batch(ps[:, 5, :]), grp(state, g), ALU.add).then_inc(c_r, 1)
                    dve.wait_ge(c_r, g + 1)
                    ln_moments(0, r_s[k], k, g + 1, c_mv, c_ve)
                if active(t, 2):
                    g, k = t - 2, u
                    dve.wait_ge(c_xw, g + 1)
                    until(dve, c_h, g - 1)
                    v.tensor_tensor(by_batch(xw_s[k]), by_batch(ps[:, 6, :]), per_batch_row(bg[:, 0, :]),
                                    ALU.add).then_inc(c_xws, 1)
                if active(t, 1):
                    g, k = t - 1, (u - 1) % 2
                    until(dve, c_tx, g - 1)
                    ln_scale(0, xn[k], r_s[k], k, g + 1, c_rs, c_xn)
                if active(t, 0):
                    dve.wait_ge(c_vd, t + 1)
                    until(dve, c_y, t - 1)
                    for c in range(EC):
                        m = v.tensor_tensor(
                            wv[u][:, c * BANK:(c + 1) * BANK].rearrange("p (h d) -> p h d", h=GH),
                            ps[:, c, :].rearrange("p (h d) -> p h d", h=GH),
                            attT[:, c, bass.ds(t * GH, GH)].rearrange("p (h o) -> p h o", o=1)
                            .broadcast_to([P, GH, DH]), ALU.mult)
                    m.then_inc(c_wv, 1)
            run_groups(dve, step_c, 3)

            def new_cell(p, i, s, c):
                n, w = unit(p, i, s, c), cols(p)
                gi, gf, gg = (gate_s[c][q][:, 0:w] for q in (GATE_I, GATE_F, GATE_G))
                cc = cell[c][:, 0:w]
                dve.wait_ge(l_in, n + 1)
                if s == 0:
                    v.tensor_tensor(cc, gi, gg, ALU.mult).then_inc(l_c, 1)
                else:
                    f = fgate(p, i, s, c)
                    v.tensor_tensor(gi, gi, gg, ALU.mult)
                    v.tensor_tensor(gf, gf, cc, ALU.mult).then_inc(l_fc, 1)
                    dve.wait_ge(l_fc, f + 1)
                    v.tensor_tensor(cc, gi, gf, ALU.add).then_inc(l_c, 1)

            def new_hidden(p, i, s, c):
                n, w = unit(p, i, s, c), cols(p)
                dve.wait_ge(l_tc, n + 1)
                dve.wait_ge(l_o, n + 1)
                if s < p - 1:
                    v.tensor_tensor(hid[c][:, 0:w], gate_s[c][GATE_O][:, 0:w], tanh_c[c][:, 0:w],
                                    ALU.mult).then_inc(l_h, 1)
                else:
                    v.tensor_tensor(at_step(p, i, c, s), windows(gate_s[c][GATE_O], p), windows(tanh_c[c], p),
                                    ALU.mult).then_inc(l_h, 1)

            def pair(p, i):
                for c in range(2):
                    new_cell(p, i, 0, c)
                for c in range(2):
                    new_hidden(p, i, 0, c)
                for s in range(1, p):
                    for c in range(2):
                        new_cell(p, i, s, c)
                        new_hidden(p, i, s, c)
            run_pairs(dve, pair)

            def step_d(t, u):
                if active(t, 2):
                    g, k = t - 2, u
                    dve.wait_ge(d_d, g + 1)
                    v.tensor_tensor(by_batch(t_s[k]), by_batch(ps[:, 0, :]), per_batch_row(b2_row[:]),
                                    ALU.add).then_inc(d_r1, 1)
                    dve.wait_ge(d_keep2, g + 1)
                    dve.wait_ge(d_r1, g + 1)
                    v.scalar_tensor_tensor(out=by_batch(t_s[k]), in0=by_batch(t_s[k]), scalar=0.0,
                                           in1=grp(state, g), op0=ALU.max, op1=ALU.add).then_inc(d_r2, 1)
                    dve.wait_ge(d_r2, g + 1)
                    v.scalar_tensor_tensor(out=by_batch(u_s[k]), in0=by_batch(t_s[k]), scalar=0.5,
                                           in1=grp(state, g), op0=ALU.mult, op1=ALU.add).then_inc(d_r3, 1)
                    dve.wait_ge(d_r3, g + 1)
                    ln_moments(1, u_s[k], k, g + 1, d_mv2, d_ve2)
                if active(t, 0):
                    dve.wait_ge(d_ts, t + 1)
                    ln_moments(0, ps[:, 2, :], u, t + 1, d_mv1, d_ve1)
                if active(t, 2):
                    g, k = t - 2, u
                    until(dve, d_tx3, g - 1)
                    until(dve, d_keep3, g - 1)
                    ln_scale(1, x3_s[k], u_s[k], k, g + 1, d_rs2, d_x3)
                if active(t, 4):
                    g, k = t - 4, u
                    dve.wait_ge(d_p, g + 1)
                    v.reciprocal(rinv[:, bass.ds(g * GRP, GRP)], rowsum[:, bass.ds(g * GRP, GRP)]).then_inc(d_ri, 1)
                    dve.wait_ge(d_ri, g + 1)
                    dve.wait_ge(d_zz, g + 1)
                    dve.wait_ge(d_keep3, g + 1)
                    for b in range(GRP):
                        m = v.scalar_tensor_tensor(
                            out=t_s[k][:, b * P:(b + 1) * P], in0=ps[:, 3, b * P:(b + 1) * P],
                            scalar=rinv[:, bass.ds(g * GRP + b, 1)],
                            in1=state[:, bass.ds(g * GRP + b, 1), :].rearrange("p o n -> p (o n)"),
                            op0=ALU.mult, op1=ALU.add)
                    m.then_inc(d_r4, 1)
                    dve.wait_ge(d_r4, g + 1)
                    ln_moments(2, t_s[k], k, g + 1, d_mv3, d_ve3)
                if active(t, 0):
                    until(dve, d_tx, t - 1)
                    until(dve, d_keep2, t - 1)
                    ln_scale(0, x2_s[u], ps[:, 2, :], u, t + 1, d_rs1, d_x2)
                if active(t, 4):
                    g, k = t - 4, u
                    if not isinstance(g, int) or g >= 2:
                        dve.wait_ge(d_out[k], (g - k) * 8)
                    ln_scale(2, o_s[k], t_s[k], k, g + 1, d_rs3, d_o)
                if active(t, 2):
                    g, k = t - 2, u
                    dve.wait_ge(d_sc, g + 1)
                    until(dve, d_p, g - 1)
                    v.tensor_tensor(by_batch(z3[k]), by_batch(ps[:, 6, :]), per_batch_row(mask[:]),
                                    ALU.add).then_inc(d_z, 1)
                    dve.wait_ge(d_z, g + 1)
                    v.tensor_reduce(nmax[:, bass.ds(g * GRP, GRP)], by_batch(z3[k]), AX_X, ALU.max,
                                    negate=True).then_inc(d_mx, 1)
            run_groups(dve, step_d, 4)


_INS = ["x", "adj", "L0_gnn_W_lin", "L0_gnn_W_val", "L0_gnn_a", "L0_gnn_W_out", "L0_gnn_src", "L0_gnn_dst",
        "L1_gnn_Wg0", "L1_gnn_bg0", "L1_gnn_Wg1", "L1_gnn_bg1", "L1_gnn_Wih", "L1_gnn_Whh", "L1_gnn_bih",
        "L1_gnn_bhh", "L2_gnn_w1_loop", "L2_gnn_w1_neigh", "L2_gnn_b1", "L2_gnn_w2_loop", "L2_gnn_w2_neigh",
        "L2_gnn_b2", "L3_gnn_Wqkv", "L3_gnn_Wo"]


def kernel(**inputs):
    import numpy as _np
    import concourse.bacc as _bacc
    from concourse import mybir as _mybir
    from concourse.bass_utils import run_bass_kernel_spmd as _run

    nc = _bacc.Bacc("TRN2", target_bir_lowering=False, num_devices=1)
    arrays, args = {}, []
    for name in _INS:
        a = _np.ascontiguousarray(inputs[name])
        arrays[f"in_{name}"] = a
        args.append(nc.dram_tensor(f"in_{name}", a.shape, _mybir.dt.from_np(a.dtype), kind="ExternalInput").ap())
    out = nc.dram_tensor("out_x", arrays["in_x"].shape, _mybir.dt.from_np(_np.dtype("float32")),
                         kind="ExternalOutput").ap()
    build(nc, *args, out)
    r = _run(nc, [arrays], core_ids=[0])
    return r.results[0]["out_x"]
```

```python
from contextlib import ExitStack

import concourse.bass as bass
from concourse import mybir

F32 = mybir.dt.float32
I32 = mybir.dt.int32
ALU = mybir.AluOpType
ACT = mybir.ActivationFunctionType
AX_X = mybir.AxisListType.X

P = 128
GRP = 4
BANK = GRP * P
LRELU_SLOPE = 0.2
LOG_EPS = 1e-8
LN_EPS = 1e-5
NEG = -1e30
RESET = 3e38
GATE_I, GATE_F, GATE_G, GATE_O = range(4)


def build(nc, x, adj, W_lin, W_val, a_att, W_out, src, dst, Wg0, bg0, Wg1, bg1, Wih, Whh, bih, bhh,
          w1_loop, w1_neigh, b1, w2_loop, w2_neigh, b2, Wqkv, Wo, out):
    B, N, D = x.shape
    HEADS, DH = a_att.shape
    E = src.shape[0]
    SKIPS = Wih.shape[0]
    NG = B // GRP
    EC = E // P
    BH = B * HEADS
    RT = BH // P
    GH = GRP * HEADS
    assert N == P and D == P and E == EC * P and BH == RT * P and EC * BH == BANK and SKIPS == 4
    SCALE = float(D) ** -0.5

    ctx = ExitStack()
    with ctx:
        def sb(name, shape, dt=F32):
            return ctx.enter_context(nc.sbuf_tensor(name, shape, dt))

        def sem(name):
            return ctx.enter_context(nc.semaphore(name))

        ps = ctx.enter_context(nc.psum_tensor("ps", [P, 8, BANK], F32))

        state = sb("state", [P, B, P])
        x1T_all = sb("x1T_all", [P, B, P])
        v_all = sb("v_all", [P, B, P])
        stage = sb("stage", [P, 20, BANK])

        ident = sb("ident", [P, P])
        ones = sb("ones", [P, P])
        eps_col = sb("eps_col", [P, 1])
        mhalf = sb("mhalf", [P, GRP])
        adj_sb = sb("adj_sb", [P, P])
        mask = sb("mask", [P, P])
        w_nat = sb("w_nat", [P, 3, P])
        wT = sb("wT", [P, 4, P])
        WoutT, adjT = wT[:, 2, :], wT[:, 3, :]
        wg = sb("wg", [P, 2, P])
        bg = sb("bg", [P, 2, P])
        w2 = sb("w2", [P, 4, P])
        b1_col = sb("b1_col", [P, 1])
        b2_col = sb("b2_col", [P, 1])
        half_b2 = sb("half_b2", [P, 1])
        w3 = sb("w3", [P, 4, P])
        w3T = sb("w3T", [P, 3, P])
        w3p = sb("w3p", [P, 2, P])
        lstm_nat = stage[:, 0:2 * SKIPS, :].rearrange("p (w s) (g h) -> p w s g h", w=2, g=4)
        lstmT = sb("lstmT", [P, 2, SKIPS, 4, P])
        lbias_nat = sb("lbias_nat", [4 * SKIPS, 2, P])
        lbias_sum = sb("lbias_sum", [4 * SKIPS, P])
        lbias = sb("lbias", [P, 4 * SKIPS])
        a_col = sb("a_col", [P, 1])
        head_of = sb("head_of", [P, HEADS])
        a_heads = sb("a_heads", [P, HEADS])

        idx_row_i = sb("idx_row_i", [P, 2, E], I32)
        idx_col_i = sb("idx_col_i", [P, 2, EC], I32)
        idx_row = sb("idx_row", [P, 2, E])
        idx_col = sb("idx_col", [P, 2, EC])
        e_row = sb("e_row", [P, E])
        e_col = sb("e_col", [P, EC])
        key_row = sb("key_row", [P, E])
        key_col = sb("key_col", [P, EC])
        rank = sb("rank", [P, EC])
        perm = sb("perm", [P, EC, E])
        idx_wide = sb("idx_wide", [P, 2, EC, P])
        sorted_row = sb("sorted_row", [P, 2, E])
        srcT = sb("srcT", [P, E])
        dstT = sb("dstT", [P, E])
        endsT = sb("endsT", [P, E])
        src_oh = sb("src_oh", [P, EC, P])
        same = sb("same", [P, E + 1])
        reset = sb("reset", [P, E + 1])
        last = sb("last", [P, E])
        adj_pick = sb("adj_pick", [P, E])
        log_adj = sb("log_adj", [P, E])
        attT = sb("attT", [P, EC, BH])

        stats = sb("stats", [P, 3, 2, GRP, 6])
        moments = sb("moments", [P, 3, 2, GRP, 2])
        var_eps = sb("var_eps", [P, 3, 2, GRP])
        rstd = sb("rstd", [P, 3, 2, GRP])
        nmean = sb("nmean", [P, 2, GRP])
        ln_bias = sb("ln_bias", [P, 2, GRP])
        nmax = sb("nmax", [P, B])
        rowsum = sb("rowsum", [P, B])
        rinv = sb("rinv", [P, B])

        s_idx, s_early, s_w, s_lw, s_x = [sem(n) for n in "s_idx s_early s_w s_lw s_x".split()]
        s_pool = sem("s_pool")
        s_dve = sem("s_dve")
        s_pe0 = sem("s_pe0")
        s_act0 = sem("s_act0")
        a_xs, a_t, a_xt, a_qv, a_q, a_v, a_g, a_z, a_l, a_e = [
            sem(n) for n in "a_xs a_t a_xt a_qv a_q a_v a_g a_z a_l a_e".split()]
        c_vd, c_wv, c_y, c_ys, c_o, c_r, c_mv, c_ve, c_rs, c_xn, c_tx, c_xt, c_all = [
            sem(n) for n in "c_vd c_wv c_y c_ys c_o c_r c_mv c_ve c_rs c_xn c_tx c_xt c_all".split()]
        c_xw, c_xws, c_h, c_hs, c_xw2, c_xw2s, c_h2, c_h2s = [
            sem(n) for n in "c_xw c_xws c_h c_hs c_xw2 c_xw2s c_h2 c_h2s".split()]
        l_gate = [sem(f"l_gate{g}") for g in range(4)]
        l_in, l_o, l_ig, l_fc, l_c, l_tc, l_h = [
            sem(n) for n in "l_in l_o l_ig l_fc l_c l_tc l_h".split()]
        (d_s, d_ts, d_mv1, d_ve1, d_rs1, d_nb1, d_x2, d_tx, d_xt, d_n1, d_n1s, d_b, d_h1, d_n2, d_n2s, d_d, d_h2,
         d_u, d_tu, d_mv2, d_ve2, d_rs2, d_x3, d_tx3, d_xt3, d_q, d_qs, d_v, d_vs, d_sc, d_z, d_mx, d_p, d_tp, d_pt,
         d_zz, d_ri, d_r4, d_mv3, d_ve3, d_rs3, d_o) = [sem(n) for n in (
             "d_s d_ts d_mv1 d_ve1 d_rs1 d_nb1 d_x2 d_tx d_xt d_n1 d_n1s d_b d_h1 d_n2 d_n2s d_d d_h2 d_u d_tu d_mv2 "
             "d_ve2 d_rs2 d_x3 d_tx3 d_xt3 d_q d_qs d_v d_vs d_sc d_z d_mx d_p d_tp d_pt d_zz d_ri d_r4 d_mv3 d_ve3 "
             "d_rs3 d_o").split()]
        d_out = [sem("d_out0"), sem("d_out1")]

        def until(eng, s, n):
            if not isinstance(n, int) or n > 0:
                eng.wait_ge(s, n)

        def run_groups(eng, step, depth):
            head = depth + 2 + depth % 2
            for t in range(head):
                step(t, t % 2)
            with eng.Fori(head, NG - 1, 2) as t:
                step(t, 0)
                step(t + 1, 1)
            for t in range(NG, NG + depth):
                step(t, t % 2)

        def active(t, offset):
            return not isinstance(t, int) or 0 <= t - offset < NG

        def grp(tile, g):
            return tile[:, bass.ds(g * GRP, GRP), :]

        def by_batch(ap):
            return ap.rearrange("p (b n) -> p b n", b=GRP)

        def per_batch_row(ap):
            return ap.rearrange("p (o n) -> p o n", o=1).broadcast_to([P, GRP, P])

        def two(first, tile=stage, n=1):
            flat = tile[:, :, :]
            return [flat[:, first + k * n:first + (k + 1) * n, :].rearrange("p s n -> p (s n)") for k in range(2)]

        v_slots = v_all[:, :, :].rearrange("p (s b) n -> p s (b n)", b=GRP)

        xs, xT, q_s = two(0), two(2), two(4)
        z_s, l_s = two(6, n=2), two(10, n=2)
        wv = two(0, n=2)
        y_s, r_s, xn, x1T, xw_s, h1_s, xw2_s = two(4), two(6), two(8), two(10), two(12), two(14), two(16)
        gate_s = [[stage[:, 4 * c + g, :] for g in range(4)] for c in range(2)]
        cell, tanh_c, hid = [[stage[:, k + c, :] for c in range(2)] for k in (8, 10, 12)]
        sum_s, x2_s, x2T, n1_s, h1T, n2_s, h2_s, uT, x3_s, x3T = [two(2 * k) for k in range(10)]
        q3, v3, z3, p3, pT, r3_s, o_s = [two(2 * k, v_slots) for k in range(7)]

        e_s = stage[:, 16, :]
        logit = stage[:, 17, :].rearrange("p (r e) -> p r e", r=RT)
        fmax = stage[:, 18, :].rearrange("p (r e) -> p r e", r=RT)
        bmax = stage[:, 19, :].rearrange("p (r e) -> p r e", r=RT)

        CHUNK = {1: GRP, 2: 2 * GRP, 3: 2 * GRP, 4: 4 * GRP}
        PAIRS = {p: B // CHUNK[p] // 2 for p in CHUNK}
        UNIT0 = {p: sum(PAIRS[q] * 2 * q for q in range(1, p)) for p in range(1, SKIPS + 2)}
        FGATE0 = {p: sum(PAIRS[q] * 2 * (q - 1) for q in range(1, p)) for p in range(1, SKIPS + 2)}
        UNITS_ALL = UNIT0[SKIPS] + PAIRS[SKIPS] * 2 * SKIPS

        def wins(p):
            return N // p

        def cols(p):
            return CHUNK[p] * wins(p)

        def at_step(p, i, c, s):
            w = wins(p)
            return state[:, bass.ds((2 * i + c) * CHUNK[p], CHUNK[p]), s:s + (w - 1) * p + 1:p]

        def windows(ap, p):
            return ap[:, 0:cols(p)].rearrange("q (b w) -> q b w", b=CHUNK[p])

        def unit(p, i, s, c):
            return UNIT0[p] + 2 * p * i + 2 * s + c

        def fgate(p, i, s, c):
            return FGATE0[p] + 2 * (p - 1) * i + 2 * (s - 1) + c

        def run_pairs(eng, pair):
            for p in range(1, SKIPS + 1):
                if p == 1:
                    pair(p, 0)
                with eng.Fori(1 if p == 1 else 0, PAIRS[p]) as i:
                    pair(p, i)

        block = ctx.enter_context(nc.Block())

        (PE_WT, PE_SORTED, PE_PICK, PE_ADJ, PE_BIAS, PE_LOGIT) = range(1, 7)
        PE_LSTM = [PE_LOGIT + 1 + k for k in range(2 * SKIPS)]
        PE_W3T, PE_W3P, PE_ATT = range(PE_LSTM[-1] + 1, PE_LSTM[-1] + 4)
        (ACT_WT, ACT_LOG, ACT_SRC) = range(1, 4)
        ACT_LSTM = ACT_SRC + 2 * SKIPS
        ACT_EXP, ACT_W3T, ACT_W3P = range(ACT_LSTM + 1, ACT_LSTM + 4)
        POOL_CONST = 7
        DV_PERM = 4 + 4 * EC
        DV_ONEHOT = DV_PERM + 4
        DV_PICK = DV_ONEHOT + 4
        DV_BIAS = DV_PICK + 1
        DV_LOGIT = DV_BIAS + 4
        DV_DIFF = DV_LOGIT + 2 * RT + 2
        DV_ATT = DV_DIFF + 3 * RT + 2
        DV_ATTT = DV_ATT + 1

        @block.sync
        def _(sp):
            as_row = lambda v: v.rearrange("(o n) -> o n", o=1)
            for k, v in enumerate((src, dst)):
                sp.dma_start(idx_row_i[:, k, :], as_row(v).broadcast_to([P, E])).then_inc(s_idx, 16)
                sp.dma_start(idx_col_i[:, k, :], v.rearrange("(c p) -> p c", c=EC),
                             allow_slow_non_contiguous=True).then_inc(s_idx, 16)
            sp.dma_start(adj_sb[:], adj).then_inc(s_early, 16)
            for k, w in enumerate((W_lin, W_val, W_out)):
                sp.dma_start(w_nat[:, k, :], w).then_inc(s_early, 16)
            sp.dma_start(a_col[:], a_att.rearrange("h (d o) -> (h d) o", o=1),
                         allow_slow_non_contiguous=True).then_inc(s_early, 16)
            xr = x.rearrange("b n d -> n b d")
            for k in range(4):
                sp.dma_start(state[:, k * B // 4:(k + 1) * B // 4, :],
                             xr[:, k * B // 4:(k + 1) * B // 4, :]).then_inc(s_x, 16)
            for k, (w, b) in enumerate(((Wg0, bg0), (Wg1, bg1))):
                sp.dma_start(wg[:, k, :], w).then_inc(s_w, 16)
                sp.dma_start(bg[:, k, :], as_row(b).broadcast_to([P, P])).then_inc(s_w, 16)
            for k, w in enumerate((w1_loop, w1_neigh, w2_loop, w2_neigh)):
                sp.dma_start(w2[:, k, :], w).then_inc(s_w, 16)
            sp.dma_start(w3[:, 0:3, :], Wqkv.rearrange("c (k n) -> c k n", k=3)).then_inc(s_w, 16)
            sp.dma_start(w3[:, 3, :], Wo).then_inc(s_w, 16)
            sp.dma_start(b1_col[:], b1.rearrange("(p o) -> p o", o=1),
                         allow_slow_non_contiguous=True).then_inc(s_w, 16)
            sp.dma_start(b2_col[:], b2.rearrange("(p o) -> p o", o=1),
                         allow_slow_non_contiguous=True).then_inc(s_w, 16)
            for k, b in enumerate((bih, bhh)):
                sp.dma_start(lbias_nat[:, k, :], b.rearrange("p (g r) -> (p g) r", g=4)).then_inc(s_w, 16)
            sp.wait_ge(a_e, NG)
            for k, w in enumerate((Wih, Whh)):
                for p in range(SKIPS):
                    sp.dma_start(lstm_nat[:, k, p], w[p].rearrange("(g r) h -> r g h", g=4)).then_inc(s_lw, 16)

            def step(t, u):
                if active(t, 4):
                    g, k = t - 4, (u - 4) % 2
                    sp.wait_ge(d_o, g + 1)
                    sp.dma_start(out[bass.ds(g * GRP, GRP)].rearrange("b n d -> n b d"),
                                 by_batch(o_s[k])).then_inc(d_out[k], 16)
            run_groups(sp, step, 4)
            for k in range(2):
                sp.wait_ge(d_out[k], 16 * NG // 2)

        @block.gpsimd
        def _(pool):
            nc.gpsimd.iota(e_row[:], pattern=[[1, E]], base=0, channel_multiplier=0,
                           allow_small_or_imprecise_dtypes=True)
            nc.gpsimd.iota(e_col[:], pattern=[[P, EC]], base=0, channel_multiplier=1,
                           allow_small_or_imprecise_dtypes=True).then_inc(s_pool, 1)
            nc.gpsimd.memset(ones[:], 1.0)
            nc.gpsimd.memset(mhalf[:], -0.5)
            nc.gpsimd.memset(head_of[:], 1.0)
            nc.gpsimd.memset(eps_col[:], LOG_EPS)
            nc.gpsimd.memset(ident[:], 0.0).then_inc(s_pool, 1)
            pool.wait_ge(s_pool, 2)
            nc.gpsimd.affine_select(out=ident[:], in_=ident[:], compare_op=ALU.not_equal, fill=1.0, base=0,
                                    pattern=[[-1, P]], channel_multiplier=1).then_inc(s_pool, 1)
            nc.gpsimd.affine_select(out=head_of[:], in_=head_of[:], compare_op=ALU.is_ge, fill=0.0, base=0,
                                    pattern=[[-DH, HEADS]], channel_multiplier=1).then_inc(s_pool, 1)
            pool.wait_ge(s_pool, 4)
            nc.gpsimd.affine_select(out=head_of[:], in_=head_of[:], compare_op=ALU.is_ge, fill=0.0, base=DH - 1,
                                    pattern=[[DH, HEADS]], channel_multiplier=-1).then_inc(s_pool, 1)
            pool.wait_ge(s_early, 5 * 16)
            nc.gpsimd.affine_select(out=mask[:], in_=adj_sb[:], compare_op=ALU.is_ge, fill=NEG, base=0,
                                    pattern=[[-1, P]], channel_multiplier=1).then_inc(s_pool, 1)
            nc.gpsimd.memset(same[:], 0.0).then_inc(s_pool, 1)

            def rstd_of(k, n, buf, s_ve, s_rs):
                pool.wait_ge(s_ve, n)
                nc.gpsimd.tensor_tensor(rstd[:, k, buf, :], var_eps[:, k, buf, :], mhalf[:], ALU.pow).then_inc(s_rs, 1)

            def step_c(t, u):
                if active(t, 1):
                    rstd_of(0, t, (u - 1) % 2, c_ve, c_rs)
            run_groups(pool, step_c, 3)

            pool.wait_ge(l_h, UNITS_ALL)

            def step_d(t, u):
                if active(t, 0):
                    until(pool, d_ts, t - 1)
                    nc.gpsimd.tensor_tensor(by_batch(sum_s[u]), grp(x1T_all, t), grp(state, t),
                                            ALU.add).then_inc(d_s, 1)
                if active(t, 0):
                    rstd_of(0, t + 1, u, d_ve1, d_rs1)
                    pool.wait_ge(d_rs1, t + 1)
                    nc.gpsimd.tensor_tensor(ln_bias[:, u, :], nmean[:, u, :], rstd[:, 0, u, :],
                                            ALU.mult).then_inc(d_nb1, 1)
                if active(t, 4):
                    rstd_of(2, t - 3, u, d_ve3, d_rs3)
                if active(t, 2):
                    rstd_of(1, t - 1, u, d_ve2, d_rs2)
            run_groups(pool, step_d, 4)

        @block.tensor
        def _(pe):
            mm = nc.tensor.matmul

            pe.wait_ge(s_pool, 3)
            pe.wait_ge(s_early, 5 * 16)
            for k in range(3):
                nc.tensor.transpose(ps[:, 0, k * P:(k + 1) * P], w_nat[:, k, :], ident[:])
            nc.tensor.transpose(ps[:, 0, 3 * P:4 * P], adj_sb[:], ident[:]).then_inc(s_pe0, 1)
            pe.wait_ge(s_dve, DV_PERM)
            for k in range(2):
                for c in range(EC):
                    m = mm(ps[:, 6, k * E:(k + 1) * E], idx_wide[:, k, c, :], perm[:, c, :],
                           start=c == 0, stop=c == EC - 1)
            m.then_inc(s_pe0, 1)
            pe.wait_ge(s_dve, DV_ONEHOT)
            mm(ps[:, 7, 0:E], adj_sb[:], srcT[:], start=True, stop=True)
            for c in range(EC):
                m = nc.tensor.transpose(ps[:, 5, c * P:(c + 1) * P], srcT[:, c * P:(c + 1) * P], ident[:])
            m.then_inc(s_pe0, 1)
            pe.wait_ge(s_dve, DV_PICK)
            mm(ps[:, 6, 0:E], ones[:], adj_pick[:], start=True, stop=True).then_inc(s_pe0, 1)
            pe.wait_ge(s_dve, DV_BIAS)
            nc.tensor.transpose(ps[:, 7, 0:4 * SKIPS], lbias_sum[:], ident[0:4 * SKIPS, 0:4 * SKIPS])\
                .then_inc(s_pe0, 1)

            pe.wait_ge(s_act0, ACT_SRC)

            def step_a(t, u):
                if active(t, 1):
                    g, k = t - 1, (u - 1) % 2
                    pe.wait_ge(a_xt, g + 1)
                    until(pe, a_q, g)
                    until(pe, a_v, g)
                    qv = ps[:, 1:3, :].rearrange("p s n -> p (s n)")
                    for b in range(GRP):
                        m = mm(qv[:, b * 2 * P:(b + 1) * 2 * P], xT[k][:, b * P:(b + 1) * P],
                               wT[:, 0:2, :].rearrange("p k n -> p (k n)"), start=True, stop=True)
                    m.then_inc(a_qv, 1)
                if active(t, 3):
                    g, k = t - 3, (u - 3) % 2
                    pe.wait_ge(a_l, g + 1)
                    for b in range(GRP):
                        for c in range(EC):
                            at = (b * EC + c) * P
                            m = mm(ps[:, 5, bass.ds(c * BH + (g * GRP + b) * HEADS, HEADS)],
                                   l_s[k][:, at:at + P], a_heads[:], start=True, stop=True)
                    m.then_inc(a_e, 1)
                if active(t, 0):
                    pe.wait_ge(a_xs, t + 1)
                    until(pe, a_xt, t)
                    for b in range(GRP):
                        m = nc.tensor.transpose(ps[:, 0, b * P:(b + 1) * P], xs[u][:, b * P:(b + 1) * P], ident[:])
                    m.then_inc(a_t, 1)
                if active(t, 2):
                    g, k = t - 2, u
                    pe.wait_ge(a_q, g + 1)
                    until(pe, a_l, g)
                    gs = ps[:, 3:5, :].rearrange("p s n -> p (s n)")
                    for b in range(GRP):
                        m = mm(gs[:, b * E:(b + 1) * E], q_s[k][:, b * P:(b + 1) * P], endsT[:],
                               start=True, stop=True)
                    m.then_inc(a_g, 1)
            run_groups(pe, step_a, 3)

            pe.wait_ge(s_dve, DV_LOGIT)
            for r in range(RT):
                for c in range(EC):
                    m = nc.tensor.transpose(ps[:, 0, r * E + c * P:r * E + (c + 1) * P],
                                            e_s[:, c * BH + r * P:c * BH + (r + 1) * P], ident[:])
            m.then_inc(s_pe0, 1)
            pe.wait_ge(s_lw, 2 * SKIPS * 16)
            for n in range(2 * SKIPS):
                if n >= 2:
                    pe.wait_ge(s_act0, ACT_SRC + n - 1)
                for q in range(4):
                    m = nc.tensor.transpose(ps[:, 1 + n % 2, q * P:(q + 1) * P],
                                            lstm_nat[:, n // SKIPS, n % SKIPS, q, :], ident[:])
                m.then_inc(s_pe0, 1)
            pe.wait_ge(s_w, 14 * 16)
            for k in range(3):
                m = nc.tensor.transpose(ps[:, 4, k * P:(k + 1) * P], w3[:, k, :], ident[:])
            m.then_inc(s_pe0, 1)
            pe.wait_ge(s_act0, ACT_W3T)
            mm(ps[:, 6, 0:P], w3T[:, 0, :], w3T[:, 1, :], start=True, stop=True)
            mm(ps[:, 6, P:2 * P], w3T[:, 2, :], w3[:, 3, :], start=True, stop=True).then_inc(s_pe0, 1)
            pe.wait_ge(s_dve, DV_ATT)
            for r in range(RT):
                for c in range(EC):
                    m = nc.tensor.transpose(ps[:, 3, c * BH + r * P:c * BH + (r + 1) * P],
                                            logit[:, r, c * P:(c + 1) * P], ident[:])
            m.then_inc(s_pe0, 1)

            pe.wait_ge(s_act0, ACT_W3P)
            pe.wait_ge(s_dve, DV_ATTT)
            pe.wait_ge(s_w, 14 * 16)

            def project(bank, src_s, w, sem_):
                for b in range(GRP):
                    m = mm(ps[:, bank, b * P:(b + 1) * P], src_s[:, b * P:(b + 1) * P], w, start=True, stop=True)
                m.then_inc(sem_, 1)

            def step_c(t, u):
                if active(t, 1):
                    g, k = t - 1, (u - 1) % 2
                    pe.wait_ge(c_wv, g + 1)
                    until(pe, c_ys, g)
                    for b in range(GRP):
                        for c in range(EC):
                            m = mm(ps[:, 2, b * P:(b + 1) * P], wv[k][:, c * BANK + b * P:c * BANK + (b + 1) * P],
                                   src_oh[:, c, :], start=c == 0, stop=c == EC - 1)
                    m.then_inc(c_y, 1)
                if active(t, 2):
                    g, k = t - 2, u
                    pe.wait_ge(c_xn, g + 1)
                    until(pe, c_hs, g)
                    for b in range(GRP):
                        m = nc.tensor.transpose(ps[:, 3, b * P:(b + 1) * P], xn[k][:, b * P:(b + 1) * P], ident[:])
                    m.then_inc(c_tx, 1)
                if active(t, 3):
                    g, k = t - 3, (u - 3) % 2
                    pe.wait_ge(c_hs, g + 1)
                    until(pe, c_xw2s, g)
                    project(4, h1_s[k], wg[:, 1, :], c_xw2)
                if active(t, 1):
                    g, k = t - 1, (u - 1) % 2
                    pe.wait_ge(c_ys, g + 1)
                    until(pe, c_r, g)
                    project(5, y_s[k], WoutT, c_o)
                if active(t, 0):
                    until(pe, c_wv, t)
                    for c in range(EC):
                        m = mm(ps[:, c, :], dstT[:, c * P:(c + 1) * P], grp(v_all, t), start=True, stop=True)
                    m.then_inc(c_vd, 1)
                if active(t, 2):
                    g, k = t - 2, u
                    pe.wait_ge(c_xt, g + 1)
                    until(pe, c_xws, g)
                    project(6, x1T[k], wg[:, 0, :], c_xw)
                if active(t, 3):
                    g, k = t - 3, (u - 3) % 2
                    pe.wait_ge(c_xw2s, g + 1)
                    until(pe, c_h2s, g)
                    project(7, xw2_s[k], adjT, c_h2)
                if active(t, 2):
                    g, k = t - 2, u
                    pe.wait_ge(c_xws, g + 1)
                    pe.wait_ge(c_all, g + 1)
                    project(3, xw_s[k], adjT, c_h)
            run_groups(pe, step_c, 3)

            pe.wait_ge(c_h2s, NG)

            def pair(p, i):
                for s in range(p):
                    gates = (GATE_I, GATE_G, GATE_O) if s == 0 else (GATE_F, GATE_I, GATE_G, GATE_O)
                    for c in range(2):
                        n = unit(p, i, s, c)
                        until(pe, l_o, n - 1)
                        if s == 0 and p == 2:
                            pe.wait_ge(l_h, UNIT0[1] + 4 * i + 2 * c + 2)
                        if s == 0 and p == 3:
                            pe.wait_ge(l_h, UNIT0[2] + 4 * i + 2 + c + 1)
                        if s == 0 and p == 4:
                            pe.wait_ge(l_h, UNIT0[3] + 12 * i + 6 * c + 6)
                        for q in gates:
                            m = mm(windows(ps[:, 4 * c + q, :], p), lstmT[:, 0, p - 1, q, :], at_step(p, i, c, s),
                                   start=True, stop=s == 0)
                            if s == 0:
                                m.then_inc(l_gate[q], 1)
                        if s > 0:
                            pe.wait_ge(l_h, n - 1)
                            for q in gates:
                                mm(ps[:, 4 * c + q, 0:cols(p)], lstmT[:, 1, p - 1, q, :], hid[c][:, 0:cols(p)],
                                   start=False, stop=True).then_inc(l_gate[q], 1)
            run_pairs(pe, pair)

            pe.wait_ge(l_o, UNITS_ALL)

            def transposes(bank, src_s, sem_):
                for b in range(GRP):
                    m = nc.tensor.transpose(ps[:, bank, b * P:(b + 1) * P], src_s[:, b * P:(b + 1) * P], ident[:])
                m.then_inc(sem_, 1)

            def graph_conv(bank, w_loop, src_T, neigh_s, s_neigh, n, sem_):
                mm(ps[:, bank, :], w_loop, src_T, start=True, stop=False, skip_group_check=True)
                pe.wait_ge(s_neigh, n)
                for b in range(GRP):
                    m = mm(ps[:, bank, b * P:(b + 1) * P], neigh_s[:, b * P:(b + 1) * P], adjT,
                           start=False, stop=b == GRP - 1, skip_group_check=True)
                m.then_inc(sem_, 1)

            def step_d(t, u):
                k1, k3 = (u - 1) % 2, (u - 3) % 2
                if active(t, 2):
                    g = t - 2
                    pe.wait_ge(d_h1, g + 1)
                    until(pe, d_r4, g - 2)
                    graph_conv(0, w2[:, 2, :], h1T[u], n2_s[u], d_n2s, g + 1, d_d)
                if active(t, 3):
                    g = t - 3
                    pe.wait_ge(d_x3, g + 1)
                    pe.wait_ge(d_n2s, min(g + 2, NG) if isinstance(t, int) else g + 2)
                    transposes(1, x3_s[k3], d_tx3)
                if active(t, 0):
                    pe.wait_ge(d_s, t + 1)
                    until(pe, d_x2, t)
                    transposes(7, sum_s[u], d_ts)
                if active(t, 1):
                    g = t - 1
                    pe.wait_ge(d_x2, g + 1)
                    until(pe, d_h1, g)
                    transposes(2, x2_s[k1], d_tx)
                if active(t, 4):
                    g = t - 4
                    pe.wait_ge(d_p, g + 1)
                    pe.wait_ge(d_vs, g + 1)
                    transposes(3, p3[u], d_tp)
                if active(t, 3):
                    g = t - 3
                    pe.wait_ge(d_xt3, g + 1)
                    until(pe, d_z, g)
                    mm(ps[:, 4, :], w3p[:, 0, :], x3T[k3], start=True, stop=True).then_inc(d_q, 1)
                if active(t, 4):
                    g = t - 4
                    pe.wait_ge(d_pt, g + 1)
                    pe.wait_ge(d_h2, min(g + 3, NG) if isinstance(t, int) else g + 3)
                    for b in range(GRP):
                        m = mm(ps[:, 0, b * P:(b + 1) * P], pT[u][:, b * P:(b + 1) * P],
                               v3[u][:, b * P:(b + 1) * P], start=True, stop=True)
                    m.then_inc(d_zz, 1)
                if active(t, 1):
                    g = t - 1
                    pe.wait_ge(d_xt, g + 1)
                    until(pe, d_n1s, g)
                    project(5, x2T[k1], w2[:, 1, :], d_n1)
                if active(t, 2):
                    g = t - 2
                    pe.wait_ge(d_u, g + 1)
                    until(pe, d_x3, g)
                    transposes(6, uT[u], d_tu)
                if active(t, 3):
                    g = t - 3
                    until(pe, d_pt, g)
                    project(3, x3T[k3], w3p[:, 1, :], d_v)
                if active(t, 1):
                    graph_conv(2, w2[:, 0, :], x2T[k1], n1_s[k1], d_n1s, t, d_b)
                if active(t, 3):
                    g = t - 3
                    pe.wait_ge(d_qs, g + 1)
                    for b in range(GRP):
                        m = mm(ps[:, 4, b * P:(b + 1) * P], q3[k3][:, b * P:(b + 1) * P],
                               x3T[k3][:, b * P:(b + 1) * P], start=True, stop=True)
                    m.then_inc(d_sc, 1)
                if active(t, 1):
                    g = t - 1
                    pe.wait_ge(d_h1, g + 1)
                    if active(t, 3):
                        pe.wait_ge(d_xt3, t - 2)
                    project(1, h1T[k1], w2[:, 3, :], d_n2)
            run_groups(pe, step_d, 4)

        @block.scalar
        def _(act):
            act.wait_ge(s_pe0, PE_WT)
            nc.scalar.copy(wT[:].rearrange("p k n -> p (k n)"), ps[:, 0, :]).then_inc(s_act0, 1)
            act.wait_ge(s_pool, 2)
            act.wait_ge(s_pe0, PE_ADJ)
            nc.scalar.activation(log_adj[:], ps[:, 6, 0:E], ACT.Ln, bias=eps_col[:]).then_inc(s_act0, 1)
            act.wait_ge(s_pe0, PE_PICK)
            nc.scalar.copy(src_oh[:].rearrange("p c n -> p (c n)"), ps[:, 5, 0:EC * P]).then_inc(s_act0, 1)

            act.wait_ge(s_x, 4 * 16)

            def step_a(t, u):
                if active(t, 0):
                    until(act, a_t, t - 1)
                    nc.scalar.copy(by_batch(xs[u]), grp(state, t)).then_inc(a_xs, 1)
                if active(t, 0):
                    act.wait_ge(a_t, t + 1)
                    until(act, a_qv, t - 1)
                    nc.scalar.copy(xT[u], ps[:, 0, :]).then_inc(a_xt, 1)
                if active(t, 2):
                    g, k = t - 2, u
                    act.wait_ge(a_g, g + 1)
                    until(act, a_l, g - 1)
                    nc.scalar.copy(z_s[k], ps[:, 3:5, :].rearrange("p s n -> p (s n)")).then_inc(a_z, 1)
            run_groups(act, step_a, 3)

            for n in range(2 * SKIPS):
                act.wait_ge(s_pe0, PE_LSTM[n])
                nc.scalar.copy(lstmT[:, n // SKIPS, n % SKIPS].rearrange("p q h -> p (q h)"),
                               ps[:, 1 + n % 2, :]).then_inc(s_act0, 1)
            act.wait_ge(s_dve, DV_DIFF)
            nc.scalar.activation(fmax[:].rearrange("p r e -> p (r e)"), logit[:].rearrange("p r e -> p (r e)"),
                                 ACT.Exp).then_inc(s_act0, 1)
            act.wait_ge(s_pe0, PE_W3T)
            nc.scalar.copy(w3T[:].rearrange("p k n -> p (k n)"), ps[:, 4, 0:3 * P]).then_inc(s_act0, 1)
            act.wait_ge(s_pe0, PE_W3P)
            nc.scalar.copy(w3p[:].rearrange("p k n -> p (k n)"), ps[:, 6, 0:2 * P]).then_inc(s_act0, 1)

            def step_c(t, u):
                if active(t, 1):
                    g, k = t - 1, (u - 1) % 2
                    act.wait_ge(c_y, g + 1)
                    until(act, c_o, g - 1)
                    nc.scalar.copy(y_s[k], ps[:, 2, :]).then_inc(c_ys, 1)
                if active(t, 2):
                    g, k = t - 2, u
                    act.wait_ge(c_tx, g + 1)
                    until(act, c_xw, g - 1)
                    nc.scalar.copy(x1T[k], ps[:, 3, :]).then_inc(c_xt, 1)
                    nc.scalar.copy(grp(x1T_all, g), by_batch(ps[:, 3, :])).then_inc(c_all, 1)
                if active(t, 3):
                    g = t - 3
                    act.wait_ge(c_h2, g + 1)
                    nc.scalar.activation(grp(state, g), by_batch(ps[:, 7, :]), ACT.Relu).then_inc(c_h2s, 1)
                if active(t, 2):
                    g, k = t - 2, u
                    act.wait_ge(c_h, g + 1)
                    until(act, c_xw2, g - 1)
                    nc.scalar.activation(h1_s[k], ps[:, 3, :], ACT.Relu).then_inc(c_hs, 1)
            run_groups(act, step_c, 3)

            def gates(p, i, s, c):
                n = unit(p, i, s, c)
                until(act, l_h, n - 1)
                for q in (GATE_I, GATE_G, GATE_O) if s == 0 else (GATE_F, GATE_I, GATE_G, GATE_O):
                    act.wait_ge(l_gate[q], fgate(p, i, s, c) + 1 if q == GATE_F else n + 1)
                    a = nc.scalar.activation(gate_s[c][q][:, 0:cols(p)], ps[:, 4 * c + q, 0:cols(p)],
                                             ACT.Tanh if q == GATE_G else ACT.Sigmoid,
                                             bias=lbias[:, 4 * (p - 1) + q:4 * (p - 1) + q + 1])
                    if q == GATE_G:
                        a.then_inc(l_in, 1)
                    if q == GATE_O:
                        a.then_inc(l_o, 1)

            def squash(p, i, s, c):
                act.wait_ge(l_c, unit(p, i, s, c) + 1)
                nc.scalar.activation(tanh_c[c][:, 0:cols(p)], cell[c][:, 0:cols(p)], ACT.Tanh).then_inc(l_tc, 1)

            def pair(p, i):
                for c in range(2):
                    gates(p, i, 0, c)
                for c in range(2):
                    squash(p, i, 0, c)
                for s in range(1, p):
                    for c in range(2):
                        gates(p, i, s, c)
                        squash(p, i, s, c)
            run_pairs(act, pair)

            def step_d(t, u):
                k1, k3 = (u - 1) % 2, (u - 3) % 2
                if active(t, 2):
                    g = t - 2
                    act.wait_ge(d_d, g + 1)
                    until(act, d_u, g - 1)
                    nc.scalar.activation(h2_s[u], ps[:, 0, :], ACT.Relu, bias=half_b2[:], scale=0.5).then_inc(d_h2, 1)
                if active(t, 3):
                    g = t - 3
                    act.wait_ge(d_tx3, g + 1)
                    until(act, d_sc, g - 1)
                    nc.scalar.copy(x3T[k3], ps[:, 1, :]).then_inc(d_xt3, 1)
                if active(t, 1):
                    g = t - 1
                    act.wait_ge(d_tx, g + 1)
                    until(act, d_u, g - 1)
                    nc.scalar.copy(x2T[k1], ps[:, 2, :]).then_inc(d_xt, 1)
                if active(t, 4):
                    g = t - 4
                    act.wait_ge(d_tp, g + 1)
                    until(act, d_zz, g - 1)
                    nc.scalar.copy(pT[u], ps[:, 3, :]).then_inc(d_pt, 1)
                if active(t, 3):
                    g = t - 3
                    act.wait_ge(d_q, g + 1)
                    nc.scalar.activation(q3[k3], ps[:, 4, :], ACT.Copy, scale=SCALE).then_inc(d_qs, 1)
                if active(t, 1):
                    g = t - 1
                    act.wait_ge(d_n1, g + 1)
                    until(act, d_b, g - 1)
                    nc.scalar.copy(n1_s[k1], ps[:, 5, :]).then_inc(d_n1s, 1)
                if active(t, 0):
                    act.wait_ge(d_nb1, t + 1)
                    until(act, d_tx, t - 1)
                    for b in range(GRP):
                        a = nc.scalar.activation(x2_s[u][:, b * P:(b + 1) * P], ps[:, 7, b * P:(b + 1) * P],
                                                 ACT.Identity, bias=ln_bias[:, u, b:b + 1],
                                                 scale=rstd[:, 0, u, b:b + 1])
                    a.then_inc(d_x2, 1)
                if active(t, 3):
                    g = t - 3
                    act.wait_ge(d_v, g + 1)
                    until(act, d_zz, g - 1)
                    nc.scalar.copy(v3[k3], ps[:, 3, :]).then_inc(d_vs, 1)
                if active(t, 1):
                    g = t - 1
                    act.wait_ge(d_b, g + 1)
                    until(act, d_d, g - 1)
                    nc.scalar.activation(h1T[k1], ps[:, 2, :], ACT.Relu, bias=b1_col[:]).then_inc(d_h1, 1)
                if active(t, 1):
                    g = t - 1
                    act.wait_ge(d_n2, g + 1)
                    nc.scalar.copy(n2_s[k1], ps[:, 1, :]).then_inc(d_n2s, 1)
                if active(t, 3):
                    g = t - 3
                    act.wait_ge(d_mx, g + 1)
                    until(act, d_tp, g - 1)
                    for b in range(GRP):
                        at = bass.ds(g * GRP + b, 1)
                        a = nc.scalar.activation(p3[k3][:, b * P:(b + 1) * P], z3[k3][:, b * P:(b + 1) * P],
                                                 ACT.Exp, bias=nmax[:, at], accum_out=rowsum[:, at])
                    a.then_inc(d_p, 1)
            run_groups(act, step_d, 4)

        @block.vector
        def _(dve):
            v = nc.vector
            count = [0]

            def link(ins):
                count[0] += 1
                ins.then_inc(s_dve, 1)
                dve.wait_ge(s_dve, count[0])

            dve.wait_ge(s_idx, 4 * 16)
            dve.wait_ge(s_pool, 1)
            link(v.tensor_copy(idx_row[:].rearrange("p k e -> p (k e)"), idx_row_i[:].rearrange("p k e -> p (k e)")))
            link(v.tensor_copy(idx_col[:].rearrange("p k c -> p (k c)"), idx_col_i[:].rearrange("p k c -> p (k c)")))
            link(v.scalar_tensor_tensor(out=key_row[:], in0=idx_row[:, 0, :], scalar=float(E), in1=e_row[:],
                                        op0=ALU.mult, op1=ALU.add))
            link(v.scalar_tensor_tensor(out=key_col[:], in0=idx_col[:, 0, :], scalar=float(E), in1=e_col[:],
                                        op0=ALU.mult, op1=ALU.add))
            for c in range(EC):
                link(v.tensor_scalar(perm[:, c, :], key_row[:], key_col[:, c:c + 1], None, ALU.is_lt, ALU.add,
                                     accum_out=rank[:, c:c + 1]))
            dve.wait_ge(s_pool, 2)
            for c in range(EC):
                link(v.tensor_scalar(perm[:, c, :], e_row[:], rank[:, c:c + 1], None, ALU.is_equal))
                for k in range(2):
                    link(v.tensor_scalar(idx_wide[:, k, c, :], ones[:], idx_col[:, k, c:c + 1], None, ALU.mult))
            assert count[0] == DV_PERM
            dve.wait_ge(s_pe0, PE_SORTED)
            link(v.tensor_copy(sorted_row[:].rearrange("p k e -> p (k e)"), ps[:, 6, :]))
            link(v.tensor_scalar(srcT[:], sorted_row[:, 0, :], e_col[:, 0:1], None, ALU.is_equal))
            link(v.tensor_scalar(dstT[:], sorted_row[:, 1, :], e_col[:, 0:1], None, ALU.is_equal))
            link(v.tensor_tensor(endsT[:], srcT[:], dstT[:], ALU.add))
            assert count[0] == DV_ONEHOT
            dve.wait_ge(s_pool, POOL_CONST)
            link(v.tensor_tensor(same[:, 1:E], sorted_row[:, 0, 1:E], sorted_row[:, 0, 0:E - 1], ALU.is_equal))
            link(v.tensor_scalar(reset[:], same[:], -1.0, RESET, ALU.add, ALU.mult))
            link(v.tensor_scalar(last[:], same[:, 1:E + 1], -1.0, 1.0, ALU.mult, ALU.add))
            dve.wait_ge(s_pe0, PE_PICK)
            link(v.tensor_tensor(adj_pick[:], ps[:, 7, 0:E], dstT[:], ALU.mult))
            assert count[0] == DV_PICK
            dve.wait_ge(s_w, 14 * 16)
            link(v.tensor_tensor(lbias_sum[:], lbias_nat[:, 0, :], lbias_nat[:, 1, :], ALU.add))
            assert count[0] == DV_BIAS
            link(v.tensor_scalar(a_heads[:], head_of[:], a_col[:], None, ALU.mult))
            link(v.tensor_scalar(half_b2[:], b2_col[:], 0.5, None, ALU.mult))
            dve.wait_ge(s_pe0, PE_BIAS)
            link(v.tensor_copy(lbias[:], ps[:, 7, 0:4 * SKIPS]))

            def step_a(t, u):
                if active(t, 1):
                    g, k = t - 1, (u - 1) % 2
                    dve.wait_ge(a_qv, g + 1)
                    until(dve, a_g, g - 1)
                    qv = ps[:, 1:3, :].rearrange("p s (b w n) -> p (s b) w n", b=GRP // 2, w=2)
                    v.tensor_copy(by_batch(q_s[k]), qv[:, :, 0, :]).then_inc(a_q, 1)
                    v.tensor_copy(grp(v_all, g), qv[:, :, 1, :]).then_inc(a_v, 1)
                if active(t, 2):
                    g, k = t - 2, u
                    dve.wait_ge(a_z, g + 1)
                    until(dve, a_e, g - 1)
                    v.scalar_tensor_tensor(out=l_s[k], in0=z_s[k], scalar=LRELU_SLOPE,
                                           in1=ps[:, 3:5, :].rearrange("p s n -> p (s n)"),
                                           op0=ALU.mult, op1=ALU.max).then_inc(a_l, 1)
            run_groups(dve, step_a, 3)

            dve.wait_ge(a_e, NG)
            link(v.tensor_copy(e_s, ps[:, 5, :]))
            assert count[0] == DV_LOGIT
            dve.wait_ge(s_pe0, PE_LOGIT)
            dve.wait_ge(s_act0, ACT_LOG)
            link(v.tensor_tensor(logit, ps[:, 0, :].rearrange("p (r e) -> p r e", r=RT),
                                 log_adj[:].rearrange("p (o e) -> p o e", o=1).broadcast_to([P, RT, E]), ALU.add))
            for r in range(RT):
                link(v.tensor_tensor_scan(fmax[:, r, :], reset[:, 0:E], logit[:, r, :], 0.0, ALU.add, ALU.max))
                link(v.tensor_tensor_scan(bmax[:, r, ::-1], reset[:, 1:E + 1][:, ::-1], fmax[:, r, ::-1], 0.0,
                                          ALU.add, ALU.max))
            link(v.tensor_tensor(logit, logit, bmax, ALU.subtract))
            assert count[0] == DV_DIFF
            dve.wait_ge(s_act0, ACT_EXP)
            for r in range(RT):
                link(v.tensor_tensor_scan(bmax[:, r, :], same[:, 0:E], fmax[:, r, :], 0.0, ALU.mult, ALU.add))
                link(v.tensor_tensor(bmax[:, r, :], bmax[:, r, :], last[:], ALU.mult))
                link(v.tensor_tensor_scan(logit[:, r, ::-1], same[:, 1:E + 1][:, ::-1], bmax[:, r, ::-1], 0.0,
                                          ALU.mult, ALU.add))
            link(v.reciprocal(bmax, logit))
            link(v.tensor_tensor(logit, fmax, bmax, ALU.mult))
            assert count[0] == DV_ATT
            dve.wait_ge(s_pe0, PE_ATT)
            link(v.tensor_copy(attT[:].rearrange("p c n -> p (c n)"), ps[:, 3, :]))
            assert count[0] == DV_ATTT

            def ln_moments(j, src_b, buf, n, s_mv, s_ve, minus_mean=None):
                for b in range(GRP):
                    v.bn_stats(stats[:, j, buf, b, :], src_b[:, b * P:(b + 1) * P])
                dve.drain()
                for b in range(GRP):
                    m = v.bn_aggr(moments[:, j, buf, b, :], stats[:, j, buf, b, :])
                m.then_inc(s_mv, 1)
                dve.wait_ge(s_mv, n)
                if minus_mean is not None:
                    v.tensor_scalar(minus_mean, moments[:, j, buf, :, 0], -1.0, None, ALU.mult)
                v.tensor_scalar(var_eps[:, j, buf, :], moments[:, j, buf, :, 1], LN_EPS, None,
                                ALU.add).then_inc(s_ve, 1)

            def ln_scale(j, dst_b, src_b, buf, n, s_rs, s_out):
                dve.wait_ge(s_rs, n)
                for b in range(GRP):
                    m = v.tensor_scalar(dst_b[:, b * P:(b + 1) * P], src_b[:, b * P:(b + 1) * P],
                                        moments[:, j, buf, b, 0:1], rstd[:, j, buf, b:b + 1],
                                        ALU.subtract, ALU.mult)
                m.then_inc(s_out, 1)

            def step_c(t, u):
                if active(t, 3):
                    g, k = t - 3, (u - 3) % 2
                    dve.wait_ge(c_xw2, g + 1)
                    until(dve, c_h2, g - 1)
                    v.tensor_tensor(by_batch(xw2_s[k]), by_batch(ps[:, 4, :]), per_batch_row(bg[:, 1, :]),
                                    ALU.add).then_inc(c_xw2s, 1)
                if active(t, 1):
                    g, k = t - 1, (u - 1) % 2
                    dve.wait_ge(c_o, g + 1)
                    v.tensor_tensor(by_batch(r_s[k]), by_batch(ps[:, 5, :]), grp(state, g), ALU.add).then_inc(c_r, 1)
                    dve.wait_ge(c_r, g + 1)
                    ln_moments(0, r_s[k], k, g + 1, c_mv, c_ve)
                if active(t, 0):
                    dve.wait_ge(c_vd, t + 1)
                    until(dve, c_y, t - 1)
                    for c in range(EC):
                        m = v.tensor_tensor(
                            wv[u][:, c * BANK:(c + 1) * BANK].rearrange("p (h d) -> p h d", h=GH),
                            ps[:, c, :].rearrange("p (h d) -> p h d", h=GH),
                            attT[:, c, bass.ds(t * GH, GH)].rearrange("p (h o) -> p h o", o=1)
                            .broadcast_to([P, GH, DH]), ALU.mult)
                    m.then_inc(c_wv, 1)
                if active(t, 2):
                    g, k = t - 2, u
                    dve.wait_ge(c_xw, g + 1)
                    until(dve, c_h, g - 1)
                    v.tensor_tensor(by_batch(xw_s[k]), by_batch(ps[:, 6, :]), per_batch_row(bg[:, 0, :]),
                                    ALU.add).then_inc(c_xws, 1)
                if active(t, 1):
                    g, k = t - 1, (u - 1) % 2
                    until(dve, c_tx, g - 1)
                    ln_scale(0, xn[k], r_s[k], k, g + 1, c_rs, c_xn)
            run_groups(dve, step_c, 3)

            def new_cell(p, i, s, c):
                n, w = unit(p, i, s, c), cols(p)
                gi, gf, gg = (gate_s[c][q][:, 0:w] for q in (GATE_I, GATE_F, GATE_G))
                cc = cell[c][:, 0:w]
                dve.wait_ge(l_in, n + 1)
                if s == 0:
                    v.tensor_tensor(cc, gi, gg, ALU.mult).then_inc(l_c, 1)
                else:
                    f = fgate(p, i, s, c)
                    v.tensor_tensor(gi, gi, gg, ALU.mult)
                    v.tensor_tensor(gf, gf, cc, ALU.mult).then_inc(l_fc, 1)
                    dve.wait_ge(l_fc, f + 1)
                    v.tensor_tensor(cc, gi, gf, ALU.add).then_inc(l_c, 1)

            def new_hidden(p, i, s, c):
                n, w = unit(p, i, s, c), cols(p)
                dve.wait_ge(l_tc, n + 1)
                dve.wait_ge(l_o, n + 1)
                if s < p - 1:
                    v.tensor_tensor(hid[c][:, 0:w], gate_s[c][GATE_O][:, 0:w], tanh_c[c][:, 0:w],
                                    ALU.mult).then_inc(l_h, 1)
                else:
                    v.tensor_tensor(at_step(p, i, c, s), windows(gate_s[c][GATE_O], p), windows(tanh_c[c], p),
                                    ALU.mult).then_inc(l_h, 1)

            def pair(p, i):
                for c in range(2):
                    new_cell(p, i, 0, c)
                for c in range(2):
                    new_hidden(p, i, 0, c)
                for s in range(1, p):
                    for c in range(2):
                        new_cell(p, i, s, c)
                        new_hidden(p, i, s, c)
            run_pairs(dve, pair)

            def step_d(t, u):
                k3 = (u - 3) % 2
                if active(t, 2):
                    g = t - 2
                    dve.wait_ge(d_h2, g + 1)
                    until(dve, d_tu, g - 1)
                    v.scalar_tensor_tensor(out=uT[u], in0=x2T[u], scalar=1.5, in1=h2_s[u],
                                           op0=ALU.mult, op1=ALU.add).then_inc(d_u, 1)
                if active(t, 0):
                    dve.wait_ge(d_ts, t + 1)
                    ln_moments(0, ps[:, 7, :], u, t + 1, d_mv1, d_ve1, nmean[:, u, :])
                if active(t, 4):
                    g = t - 4
                    dve.wait_ge(d_p, g + 1)
                    v.reciprocal(rinv[:, bass.ds(g * GRP, GRP)], rowsum[:, bass.ds(g * GRP, GRP)]).then_inc(d_ri, 1)
                    dve.wait_ge(d_ri, g + 1)
                    dve.wait_ge(d_zz, g + 1)
                    for b in range(GRP):
                        m = v.scalar_tensor_tensor(
                            out=r3_s[u][:, b * P:(b + 1) * P], in0=ps[:, 0, b * P:(b + 1) * P],
                            scalar=rinv[:, bass.ds(g * GRP + b, 1)], in1=x3_s[u][:, b * P:(b + 1) * P],
                            op0=ALU.mult, op1=ALU.add)
                    m.then_inc(d_r4, 1)
                    dve.wait_ge(d_r4, g + 1)
                    ln_moments(2, r3_s[u], u, g + 1, d_mv3, d_ve3)
                if active(t, 2):
                    g = t - 2
                    dve.wait_ge(d_tu, g + 1)
                    ln_moments(1, ps[:, 6, :], u, g + 1, d_mv2, d_ve2)
                if active(t, 4):
                    g = t - 4
                    if not isinstance(g, int) or g >= 2:
                        dve.wait_ge(d_out[u], (g - u) * 8)
                    ln_scale(2, o_s[u], r3_s[u], u, g + 1, d_rs3, d_o)
                if active(t, 3):
                    g = t - 3
                    dve.wait_ge(d_sc, g + 1)
                    until(dve, d_p, g - 1)
                    v.tensor_tensor(by_batch(z3[k3]), by_batch(ps[:, 4, :]), per_batch_row(mask[:]),
                                    ALU.add).then_inc(d_z, 1)
                    dve.wait_ge(d_z, g + 1)
                    v.tensor_reduce(nmax[:, bass.ds(g * GRP, GRP)], by_batch(z3[k3]), AX_X, ALU.max,
                                    negate=True).then_inc(d_mx, 1)
                if active(t, 2):
                    g = t - 2
                    until(dve, d_tx3, g - 1)
                    ln_scale(1, x3_s[u], ps[:, 6, :], u, g + 1, d_rs2, d_x3)
            run_groups(dve, step_d, 4)


_INS = ["x", "adj", "L0_gnn_W_lin", "L0_gnn_W_val", "L0_gnn_a", "L0_gnn_W_out", "L0_gnn_src", "L0_gnn_dst",
        "L1_gnn_Wg0", "L1_gnn_bg0", "L1_gnn_Wg1", "L1_gnn_bg1", "L1_gnn_Wih", "L1_gnn_Whh", "L1_gnn_bih",
        "L1_gnn_bhh", "L2_gnn_w1_loop", "L2_gnn_w1_neigh", "L2_gnn_b1", "L2_gnn_w2_loop", "L2_gnn_w2_neigh",
        "L2_gnn_b2", "L3_gnn_Wqkv", "L3_gnn_Wo"]


def kernel(**inputs):
    import numpy as _np
    import concourse.bacc as _bacc
    from concourse import mybir as _mybir
    from concourse.bass_utils import run_bass_kernel_spmd as _run

    nc = _bacc.Bacc("TRN2", target_bir_lowering=False, num_devices=1)
    arrays, args = {}, []
    for name in _INS:
        a = _np.ascontiguousarray(inputs[name])
        arrays[f"in_{name}"] = a
        args.append(nc.dram_tensor(f"in_{name}", a.shape, _mybir.dt.from_np(a.dtype), kind="ExternalInput").ap())
    out = nc.dram_tensor("out_x", arrays["in_x"].shape, _mybir.dt.from_np(_np.dtype("float32")),
                         kind="ExternalOutput").ap()
    build(nc, *args, out)
    r = _run(nc, [arrays], core_ids=[0])
    return r.results[0]["out_x"]
```

```python
from contextlib import ExitStack

import concourse.bass as bass
from concourse import mybir

F32 = mybir.dt.float32
F32R = mybir.dt.float32r
BF16 = mybir.dt.bfloat16
I32 = mybir.dt.int32
ALU = mybir.AluOpType
ACT = mybir.ActivationFunctionType
AX_X = mybir.AxisListType.X

P = 128
GRP = 4
BANK = GRP * P
LRELU_SLOPE = 0.2
LOG_EPS = 1e-8
LN_EPS = 1e-5
NEG = -1e30
RESET = 3e38
GATE_I, GATE_F, GATE_G, GATE_O = range(4)
GATE_BANK = (0, 3, 1, 2)


def build(nc, x, adj, W_lin, W_val, a_att, W_out, src, dst, Wg0, bg0, Wg1, bg1, Wih, Whh, bih, bhh,
          w1_loop, w1_neigh, b1, w2_loop, w2_neigh, b2, Wqkv, Wo, out):
    B, N, D = x.shape
    HEADS, DH = a_att.shape
    E = src.shape[0]
    SKIPS = Wih.shape[0]
    NG = B // GRP
    EC = E // P
    BH = B * HEADS
    RT = BH // P
    GH = GRP * HEADS
    assert N == P and D == P and E == EC * P and BH == RT * P and EC * BH == BANK and SKIPS == 4 and RT == 2 and NG > 4
    SCALE = float(D) ** -0.5

    ctx = ExitStack()
    with ctx:
        def sb(name, shape, dt=F32):
            return ctx.enter_context(nc.sbuf_tensor(name, shape, dt))

        def sem(name):
            return ctx.enter_context(nc.semaphore(name))

        ps = ctx.enter_context(nc.psum_tensor("ps", [P, 8, BANK], F32))

        def next_at():
            return -(-nc.sbuf_base // 32) * 32

        def over(first, name, shape, dt=F32):
            return nc.alloc_sbuf_tensor_at(name, shape, dt, offset=first)


        state_at = next_at()
        state = sb("state", [P, B, P])
        h_lo = over(state_at, "h_lo", [P, B, P], F32R)
        v_at = next_at()
        v_hi = sb("v_hi", [P, B, P], F32R)
        h_hi = over(v_at, "h_hi", [P, B, P], F32R)
        x1T_at = next_at()
        v_lo = sb("v_lo", [P, B, P], F32R)
        x1T_all = over(x1T_at, "x1T_all", [P, B, P])
        stage_at = next_at()
        stage = sb("stage", [P, 20, BANK])
        hid_hi = over(stage_at + 14 * BANK * 4, "hid_hi", [P, 2, BANK], F32R)
        hid_lo = over(stage_at + 16 * BANK * 4, "hid_lo", [P, 2, BANK], F32R)

        ident = sb("ident", [P, P])
        ones = sb("ones", [P, P])
        eps_col = sb("eps_col", [P, 1])
        mhalf = sb("mhalf", [P, GRP])
        adj_sb = sb("adj_sb", [P, P])
        mask = sb("mask", [P, P])
        w_nat = sb("w_nat", [P, 3, P])
        wT = sb("wT", [P, 4, P])
        WoutT, adjT = wT[:, 2, :], wT[:, 3, :]
        wg = sb("wg", [P, 2, P])
        bg = sb("bg", [P, 2, P])
        w2 = sb("w2", [P, 4, P])
        b1_col = sb("b1_col", [P, 1])
        b2_col = sb("b2_col", [P, 1])
        half_b2 = sb("half_b2", [P, 1])
        w3 = sb("w3", [P, 4, P])
        w3T = sb("w3T", [P, 3, P])
        w3p = sb("w3p", [P, 2, P])
        lstm_at = next_at()
        lstm_hi = sb("lstm_hi", [P, 2, SKIPS, 4, P], F32R)
        lstm_lo_at = next_at()
        lstm_lo = sb("lstm_lo", [P, 2, SKIPS, 4, P], F32R)
        lstm_nat = over(lstm_lo_at, "lstm_nat", [P, 2, SKIPS, 4, P])
        lstm_t = over(stage_at, "lstm_t", [P, 2, BANK])
        stage_d = over(lstm_at, "stage_d", [P, 16, BANK])
        lbias_nat = sb("lbias_nat", [4 * SKIPS, 2, P])
        lbias_sum = sb("lbias_sum", [4 * SKIPS, P])
        lbias = sb("lbias", [P, 4 * SKIPS])
        a_col = sb("a_col", [P, 1])
        head_of = sb("head_of", [P, HEADS])
        a_heads = sb("a_heads", [P, HEADS])

        idx_row_i = sb("idx_row_i", [P, 2, E], I32)
        idx_col_i = sb("idx_col_i", [P, 2, EC], I32)
        idx_row = sb("idx_row", [P, 2, E])
        idx_col = sb("idx_col", [P, 2, EC])
        e_row = sb("e_row", [P, E])
        e_col = sb("e_col", [P, EC])
        key_row = sb("key_row", [P, E])
        key_col = sb("key_col", [P, EC])
        rank = sb("rank", [P, EC])
        edges_at = stage_at + 18 * BANK * 4
        perm = over(edges_at, "perm", [P, EC, E], BF16)
        idx_wide = over(edges_at + EC * E * 2, "idx_wide", [P, 2, EC, P], BF16)
        sorted_row = sb("sorted_row", [P, 2, E])
        srcT = sb("srcT", [P, E])
        dstT = sb("dstT", [P, E], F32R)
        endsT = sb("endsT", [P, E], F32R)
        src_oh = sb("src_oh", [P, EC, P])
        same = sb("same", [P, E + 1])
        reset = sb("reset", [P, E + 1])
        last = sb("last", [P, E])
        adj_pick = sb("adj_pick", [P, E])
        log_adj = sb("log_adj", [P, E])
        attT = sb("attT", [P, EC, BH])

        stats = sb("stats", [P, 3, 2, GRP, 6])
        moments = sb("moments", [P, 3, 2, GRP, 2])
        var_eps = sb("var_eps", [P, 3, 2, GRP])
        rstd = sb("rstd", [P, 3, 2, GRP])
        nmean = sb("nmean", [P, 2, GRP])
        ln_bias = sb("ln_bias", [P, 2, GRP])
        nmax = sb("nmax", [P, B])
        rowsum = sb("rowsum", [P, B])
        rinv = sb("rinv", [P, B])

        s_idx, s_early, s_w, s_lw = [sem(n) for n in "s_idx s_early s_w s_lw".split()]
        s_x = [sem(f"s_x{k}") for k in range(4)]
        s_pool = sem("s_pool")
        s_dve = sem("s_dve")
        s_pe0 = sem("s_pe0")
        s_lo = sem("s_lo")
        s_act0 = sem("s_act0")
        a_xs, a_t, a_xt, a_qv, a_hi, a_q, a_v, a_g, a_z, a_l, a_e = [
            sem(n) for n in "a_xs a_t a_xt a_qv a_hi a_q a_v a_g a_z a_l a_e".split()]
        c_vd, c_wv, c_y, c_ys, c_o, c_r, c_mv, c_ve, c_rs, c_nb, c_xn, c_tx, c_xt, c_all = [
            sem(n) for n in "c_vd c_wv c_y c_ys c_o c_r c_mv c_ve c_rs c_nb c_xn c_tx c_xt c_all".split()]
        c_xw, c_xws, c_h, c_hs, c_xw2, c_xw2s, c_h2, c_h2s, c_hl = [
            sem(n) for n in "c_xw c_xws c_h c_hs c_xw2 c_xw2s c_h2 c_h2s c_hl".split()]
        l_gate = [sem(f"l_gate{g}") for g in range(4)]
        l_i, l_in, l_o, l_fc, l_c, l_tc, l_hh, l_h = [
            sem(n) for n in "l_i l_in l_o l_fc l_c l_tc l_hh l_h".split()]
        (d_h, d_s, d_ts, d_mv1, d_ve1, d_rs1, d_nb1, d_x2, d_tx, d_xt, d_n1, d_n1s, d_b, d_h1, d_n2, d_n2s, d_d, d_h2,
         d_u, d_tu, d_mv2, d_ve2, d_rs2, d_x3, d_tx3, d_xt3, d_q, d_qs, d_v, d_vs, d_sc, d_z, d_mx, d_p, d_tp, d_pt,
         d_zz, d_ri, d_r4, d_mv3, d_ve3, d_rs3, d_o) = [sem(n) for n in (
             "d_h d_s d_ts d_mv1 d_ve1 d_rs1 d_nb1 d_x2 d_tx d_xt d_n1 d_n1s d_b d_h1 d_n2 d_n2s d_d d_h2 d_u d_tu "
             "d_mv2 d_ve2 d_rs2 d_x3 d_tx3 d_xt3 d_q d_qs d_v d_vs d_sc d_z d_mx d_p d_tp d_pt d_zz d_ri d_r4 d_mv3 "
             "d_ve3 d_rs3 d_o").split()]
        d_out = [sem("d_out0"), sem("d_out1")]

        def until(eng, s, n):
            if not isinstance(n, int) or n > 0:
                eng.wait_ge(s, n)

        def run_groups(eng, step, depth):
            head = depth + 2 + depth % 2
            for t in range(head):
                step(t, t % 2)
            with eng.Fori(head, NG - 1, 2) as t:
                step(t, 0)
                step(t + 1, 1)
            for t in range(NG, NG + depth):
                step(t, t % 2)

        def active(t, offset):
            return not isinstance(t, int) or 0 <= t - offset < NG

        def grp(tile, g):
            return tile[:, bass.ds(g * GRP, GRP), :]

        def by_batch(ap):
            return ap.rearrange("p (b n) -> p b n", b=GRP)

        def per_batch_row(ap):
            return ap.rearrange("p (o n) -> p o n", o=1).broadcast_to([P, GRP, P])

        def two(first, tile=stage, n=1):
            flat = tile[:, :, :]
            return [flat[:, first + k * n:first + (k + 1) * n, :].rearrange("p s n -> p (s n)") for k in range(2)]

        xs, xT = two(0), two(2)
        q_hi = over(stage_at + 4 * BANK * 4, "q_hi", [P, 2, BANK], F32R)
        q_lo = over(stage_at + 14 * BANK * 4, "q_lo", [P, 2, BANK], F32R)
        z_s, l_s = two(6, n=2), two(10, n=2)
        wv = two(0, n=2)
        y_s, r_s, xn, x1T, xw_s, h1_s, xw2_s = two(4), two(6), two(8), two(10), two(12), two(14), two(16)
        gate_s = [[stage[:, 4 * c + g, :] for g in range(4)] for c in range(2)]
        first_o = [stage[:, 18 + c, :] for c in range(2)]
        cell, tanh_c, hid = [[stage[:, k + c, :] for c in range(2)] for k in (8, 10, 12)]
        o_s, x2_s, x2T, n1_s, h1T, n2_s, h2_s, uT, x3_s, x3T = [two(2 * k) for k in range(10)]
        h_s, q3, sum_s, v3, z3, p3, pT, r3_s = [two(2 * k, stage_d) for k in range(8)]

        e_s = stage[:, 16, :]
        logit = stage[:, 17, :].rearrange("p (r e) -> p r e", r=RT)
        fmax = stage[:, 18, :].rearrange("p (r e) -> p r e", r=RT)
        bmax = stage[:, 19, :].rearrange("p (r e) -> p r e", r=RT)

        CHUNK = {1: GRP, 2: 2 * GRP, 3: 2 * GRP, 4: 4 * GRP}
        PAIRS = {p: B // CHUNK[p] // 2 for p in CHUNK}
        BODY0 = {2: 2 * PAIRS[1] + 2}
        for p in range(2, SKIPS):
            BODY0[p + 1] = BODY0[p] + 2 * p * PAIRS[p]
        FGATE0 = {p: sum(PAIRS[q] * 2 * (q - 1) for q in range(1, p)) for p in range(1, SKIPS + 1)}
        UNITS_ALL = sum(PAIRS[p] * 2 * p for p in CHUNK)

        def wins(p):
            return N // p

        def cols(p):
            return CHUNK[p] * wins(p)

        def at_step(tile, p, i, c, s):
            w = wins(p)
            return tile[:, bass.ds((2 * i + c) * CHUNK[p], CHUNK[p]), s:s + (w - 1) * p + 1:p]

        def is_start(p, i, s):
            return p == 2 and s == 0 and isinstance(i, int) and i == 0

        def gate_tile(c, q, s):
            return first_o[c] if q == GATE_O and s == 0 else gate_s[c][q]

        def windows(ap, p):
            return ap[:, 0:cols(p)].rearrange("q (b w) -> q b w", b=CHUNK[p])

        def is_last_pair_1(i):
            return isinstance(i, int) and i == PAIRS[1] - 1

        def unit(p, i, s, c):
            if p == 1:
                return 2 * i + (2 * c if is_last_pair_1(i) else c)
            if s == 0:
                return BODY0[p] + 2 * p * i - 3 + 2 * c
            followed = s == p - 1 and not (p == SKIPS and isinstance(i, int) and i == PAIRS[p] - 1)
            return BODY0[p] + 2 * p * i + 2 * (s - 1) + (2 * c if followed else c)

        def before(p, i, s, c):
            if s > 0:
                return unit(p, i, s - 1, c) + 1
            return unit(p, i, 0, c) - (0 if p > 1 else 1 + c if is_last_pair_1(i) else 1)

        def fgate(p, i, s, c):
            return FGATE0[p] + 2 * (p - 1) * i + 2 * (s - 1) + c

        def run_units(eng, starts, step):
            with eng.Fori(2, PAIRS[1] - 1) as i:
                starts(1, i)
            for c in range(2):
                step(1, PAIRS[1] - 1, 0, c, (2, 0))

            def body(p, i, following):
                for s in range(1, p):
                    for c in range(2):
                        step(p, i, s, c, following if s == p - 1 else None)

            for p in range(2, SKIPS + 1):
                with eng.Fori(0, PAIRS[p] - 1) as i:
                    body(p, i, (p, i + 1))
                body(p, PAIRS[p] - 1, (p + 1, 0) if p < SKIPS else None)

        block = ctx.enter_context(nc.Block())

        PE_WT, PE_SORTED, PE_PICK, PE_ADJ = range(1, 5)
        PE_LSTM = [PE_ADJ + 1 + k for k in range(2 * SKIPS)]
        PE_LOGIT, PE_W3T, PE_W3P, *PE_ATT = range(PE_LSTM[-1] + 1, PE_LSTM[-1] + 4 + RT)
        ACT_WT, ACT_LOG, ACT_SRC = range(1, 4)
        ACT_LSTM = [ACT_SRC + 1 + k for k in range(2 * SKIPS)]
        ACT_W3T, ACT_LBIAS, *ACT_EXP, ACT_W3P = range(ACT_LSTM[-1] + 1, ACT_LSTM[-1] + 4 + RT)
        POOL_CONST = 7
        DV_PERM = 4 + 4 * EC
        DV_ONEHOT = DV_PERM + 4
        DV_HEADS = DV_ONEHOT + 1
        DV_PICK = DV_HEADS + 4
        DV_BIAS = DV_PICK + 2
        DV_LOGIT = DV_BIAS + 1
        DV_DIFF = [DV_LOGIT + 4 * (k + 1) for k in range(RT)]
        DV_ATT = [DV_DIFF[-1] + 6 * k + 5 for k in range(RT)]
        DV_ATTT = [n + 1 for n in DV_ATT]
        A_PICK, A_ADJ = 4, 5
        A_LSTM = {NG: (0, 1, 2), NG + 1: (3, 4, 5), NG + 2: (6, 7)}

        def is_step(t, step):
            return isinstance(t, int) and t == step

        def lstm_at_step(t):
            return A_LSTM.get(t, ()) if isinstance(t, int) else ()

        @block.sync
        def _(sp):
            as_row = lambda v: v.rearrange("(o n) -> o n", o=1)
            for k, v in enumerate((src, dst)):
                sp.dma_start(idx_row_i[:, k, :], as_row(v).broadcast_to([P, E])).then_inc(s_idx, 16)
                sp.dma_start(idx_col_i[:, k, :], v.rearrange("(c p) -> p c", c=EC),
                             allow_slow_non_contiguous=True).then_inc(s_idx, 16)
            sp.dma_start(adj_sb[:], adj).then_inc(s_early, 16)
            for k, w in enumerate((W_lin, W_val, W_out)):
                sp.dma_start(w_nat[:, k, :], w).then_inc(s_early, 16)
            sp.dma_start(a_col[:], a_att.rearrange("h (d o) -> (h d) o", o=1),
                         allow_slow_non_contiguous=True).then_inc(s_early, 16)
            xr = x.rearrange("b n d -> n b d")
            for k in range(4):
                sp.dma_start(state[:, k * B // 4:(k + 1) * B // 4, :],
                             xr[:, k * B // 4:(k + 1) * B // 4, :]).then_inc(s_x[k], 16)
            for k, (w, b) in enumerate(((Wg0, bg0), (Wg1, bg1))):
                sp.dma_start(wg[:, k, :], w).then_inc(s_w, 16)
                sp.dma_start(bg[:, k, :], as_row(b).broadcast_to([P, P])).then_inc(s_w, 16)
            for k, w in enumerate((w1_loop, w1_neigh, w2_loop, w2_neigh)):
                sp.dma_start(w2[:, k, :], w).then_inc(s_w, 16)
            sp.dma_start(w3[:, 0:3, :], Wqkv.rearrange("c (k n) -> c k n", k=3)).then_inc(s_w, 16)
            sp.dma_start(w3[:, 3, :], Wo).then_inc(s_w, 16)
            sp.dma_start(b1_col[:], b1.rearrange("(p o) -> p o", o=1),
                         allow_slow_non_contiguous=True).then_inc(s_w, 16)
            sp.dma_start(b2_col[:], b2.rearrange("(p o) -> p o", o=1),
                         allow_slow_non_contiguous=True).then_inc(s_w, 16)
            for k, b in enumerate((bih, bhh)):
                sp.dma_start(lbias_nat[:, k, :], b.rearrange("p (g r) -> (p g) r", g=4)).then_inc(s_w, 16)
            for k, w in enumerate((Wih, Whh)):
                for p in range(SKIPS):
                    sp.dma_start(lstm_nat[:, k, p], w[p].rearrange("(g r) h -> r g h", g=4)).then_inc(s_lw, 16)

            def step(t, u):
                if active(t, 4):
                    g, k = t - 4, (u - 4) % 2
                    sp.wait_ge(d_o, g + 1)
                    sp.dma_start(out[bass.ds(g * GRP, GRP)].rearrange("b n d -> n b d"),
                                 by_batch(o_s[k])).then_inc(d_out[k], 16)
            run_groups(sp, step, 4)
            for k in range(2):
                sp.wait_ge(d_out[k], 16 * NG // 2)

        @block.gpsimd
        def _(pool):
            nc.gpsimd.iota(e_row[:], pattern=[[1, E]], base=0, channel_multiplier=0,
                           allow_small_or_imprecise_dtypes=True)
            nc.gpsimd.iota(e_col[:], pattern=[[P, EC]], base=0, channel_multiplier=1,
                           allow_small_or_imprecise_dtypes=True).then_inc(s_pool, 1)
            nc.gpsimd.memset(ones[:], 1.0)
            nc.gpsimd.memset(mhalf[:], -0.5)
            nc.gpsimd.memset(head_of[:], 1.0)
            nc.gpsimd.memset(eps_col[:], LOG_EPS)
            nc.gpsimd.memset(ident[:], 0.0).then_inc(s_pool, 1)
            pool.wait_ge(s_pool, 2)
            nc.gpsimd.affine_select(out=ident[:], in_=ident[:], compare_op=ALU.not_equal, fill=1.0, base=0,
                                    pattern=[[-1, P]], channel_multiplier=1).then_inc(s_pool, 1)
            nc.gpsimd.affine_select(out=head_of[:], in_=head_of[:], compare_op=ALU.is_ge, fill=0.0, base=0,
                                    pattern=[[-DH, HEADS]], channel_multiplier=1).then_inc(s_pool, 1)
            pool.wait_ge(s_pool, 4)
            nc.gpsimd.affine_select(out=head_of[:], in_=head_of[:], compare_op=ALU.is_ge, fill=0.0, base=DH - 1,
                                    pattern=[[DH, HEADS]], channel_multiplier=-1).then_inc(s_pool, 1)
            pool.wait_ge(s_early, 5 * 16)
            nc.gpsimd.affine_select(out=mask[:], in_=adj_sb[:], compare_op=ALU.is_ge, fill=NEG, base=0,
                                    pattern=[[-1, P]], channel_multiplier=1).then_inc(s_pool, 1)
            nc.gpsimd.memset(same[:], 0.0).then_inc(s_pool, 1)

            def rstd_of(k, n, buf, s_ve, s_rs):
                pool.wait_ge(s_ve, n)
                nc.gpsimd.tensor_tensor(rstd[:, k, buf, :], var_eps[:, k, buf, :], mhalf[:], ALU.pow).then_inc(s_rs, 1)

            for n in range(2 * SKIPS):
                pool.wait_ge(s_act0, ACT_LSTM[n])
                nc.gpsimd.tensor_tensor(lstm_lo[:, n // SKIPS, n % SKIPS].rearrange("p q h -> p (q h)"),
                                        lstm_t[:, n % 2, :],
                                        lstm_hi[:, n // SKIPS, n % SKIPS].rearrange("p q h -> p (q h)"),
                                        ALU.subtract).then_inc(s_lo, 1)

            def step_c(t, u):
                if active(t, 1):
                    rstd_of(0, t, (u - 1) % 2, c_ve, c_rs)
                    pool.wait_ge(c_rs, t)
                    nc.gpsimd.tensor_tensor(ln_bias[:, (u - 1) % 2, :], nmean[:, (u - 1) % 2, :],
                                            rstd[:, 0, (u - 1) % 2, :], ALU.mult).then_inc(c_nb, 1)
            run_groups(pool, step_c, 4)

            def starts_l(i):
                for c in range(2):
                    pool.wait_ge(l_hh, unit(1, i, 0, c) + 1)
                    nc.gpsimd.tensor_tensor(at_step(h_lo, 1, i, c, 0), windows(hid[c], 1), at_step(h_hi, 1, i, c, 0),
                                            ALU.subtract).then_inc(l_h, 1)
            starts_l(0)
            starts_l(1)
            with pool.Fori(2, PAIRS[1] - 1) as i:
                starts_l(i)

            def step_d(t, u):
                if active(t, 0):
                    if is_step(t, 0):
                        pool.wait_ge(l_h, unit(4, 0, 3, 0) + 1)
                    if is_step(t, 4):
                        pool.wait_ge(l_h, UNITS_ALL)
                    until(pool, d_ts, t - 1)
                    nc.gpsimd.tensor_tensor(by_batch(h_s[u]), grp(h_hi, t), grp(h_lo, t), ALU.add).then_inc(d_h, 1)
                    pool.wait_ge(d_h, t + 1)
                    nc.gpsimd.tensor_tensor(by_batch(sum_s[u]), grp(x1T_all, t), by_batch(h_s[u]),
                                            ALU.add).then_inc(d_s, 1)
                if active(t, 2):
                    rstd_of(0, t - 1, u, d_ve1, d_rs1)
                    pool.wait_ge(d_rs1, t - 1)
                    nc.gpsimd.tensor_tensor(ln_bias[:, u, :], nmean[:, u, :], rstd[:, 0, u, :],
                                            ALU.mult).then_inc(d_nb1, 1)
                if active(t, 6):
                    rstd_of(2, t - 5, u, d_ve3, d_rs3)
                if active(t, 4):
                    rstd_of(1, t - 3, u, d_ve2, d_rs2)
            run_groups(pool, step_d, 6)

        @block.tensor
        def _(pe):
            mm = nc.tensor.matmul

            pe.wait_ge(s_pool, 3)
            pe.wait_ge(s_early, 5 * 16)
            for k in range(3):
                nc.tensor.transpose(ps[:, 0, k * P:(k + 1) * P], w_nat[:, k, :], ident[:])
            nc.tensor.transpose(ps[:, 0, 3 * P:4 * P], adj_sb[:], ident[:]).then_inc(s_pe0, 1)
            pe.wait_ge(s_dve, DV_PERM)
            for k in range(2):
                for c in range(EC):
                    m = mm(ps[:, 6, k * E:(k + 1) * E], idx_wide[:, k, c, :], perm[:, c, :],
                           start=c == 0, stop=c == EC - 1)
            m.then_inc(s_pe0, 1)
            pe.wait_ge(s_act0, ACT_WT)

            def step_a(t, u):
                if active(t, 1):
                    g, k = t - 1, (u - 1) % 2
                    pe.wait_ge(a_xt, g + 1)
                    until(pe, a_q, g)
                    until(pe, a_v, g)
                    qv = ps[:, 1:3, :].rearrange("p s n -> p (s n)")
                    for b in range(GRP):
                        m = mm(qv[:, b * 2 * P:(b + 1) * 2 * P], xT[k][:, b * P:(b + 1) * P],
                               wT[:, 0:2, :].rearrange("p k n -> p (k n)"), start=True, stop=True)
                    m.then_inc(a_qv, 1)
                if active(t, 0):
                    pe.wait_ge(a_xs, t + 1)
                    until(pe, a_xt, t)
                    for b in range(GRP):
                        m = nc.tensor.transpose(ps[:, 0, b * P:(b + 1) * P], xs[u][:, b * P:(b + 1) * P], ident[:])
                    m.then_inc(a_t, 1)
                if active(t, 2):
                    g, k = t - 2, u
                    if is_step(t, 2):
                        pe.wait_ge(s_dve, DV_ONEHOT)
                    pe.wait_ge(a_q, g + 1)
                    until(pe, a_l, g)
                    gs = ps[:, 3:5, :].rearrange("p s n -> p (s n)")
                    for b in range(GRP):
                        for q in (q_hi, q_lo):
                            m = mm(gs[:, b * E:(b + 1) * E], q[:, k, b * P:(b + 1) * P], endsT[:],
                                   start=q is q_hi, stop=q is q_lo)
                    m.then_inc(a_g, 1)
                if active(t, 3):
                    g, k = t - 3, (u - 3) % 2
                    if is_step(t, 3):
                        pe.wait_ge(s_dve, DV_HEADS)
                    pe.wait_ge(a_l, g + 1)
                    for b in range(GRP):
                        for c in range(EC):
                            at = (b * EC + c) * P
                            m = mm(ps[:, 5, bass.ds(c * BH + (g * GRP + b) * HEADS, HEADS)],
                                   l_s[k][:, at:at + P], a_heads[:], start=True, stop=True)
                    m.then_inc(a_e, 1)
                if is_step(t, A_PICK):
                    mm(ps[:, 7, 0:E], adj_sb[:], srcT[:], start=True, stop=True).then_inc(s_pe0, 1)
                if is_step(t, A_ADJ):
                    for c in range(EC):
                        nc.tensor.transpose(ps[:, 6, E + c * P:E + (c + 1) * P], srcT[:, c * P:(c + 1) * P], ident[:])
                    pe.wait_ge(s_dve, DV_PICK)
                    mm(ps[:, 6, 0:E], ones[:], adj_pick[:], start=True, stop=True).then_inc(s_pe0, 1)
                if is_step(t, NG):
                    pe.wait_ge(s_lw, 2 * SKIPS * 16)
                for n in lstm_at_step(t):
                    pe.wait_ge(s_act0, ACT_LSTM[n - 2] if n >= 2 else ACT_SRC)
                    for q in range(4):
                        m = nc.tensor.transpose(ps[:, 6 + n % 2, q * P:(q + 1) * P],
                                                lstm_nat[:, n // SKIPS, n % SKIPS, q, :], ident[:])
                    m.then_inc(s_pe0, 1)
            run_groups(pe, step_a, 3)

            def gather_values(g):
                for c in range(EC):
                    for part in (v_hi, v_lo):
                        m = mm(ps[:, c, :], dstT[:, c * P:(c + 1) * P], grp(part, g),
                               start=part is v_hi, stop=part is v_lo)
                m.then_inc(c_vd, 1)

            pe.wait_ge(s_dve, DV_LOGIT)
            for r in range(RT):
                for c in range(EC):
                    m = nc.tensor.transpose(ps[:, 0, r * E + c * P:r * E + (c + 1) * P],
                                            e_s[:, c * BH + r * P:c * BH + (r + 1) * P], ident[:])
            m.then_inc(s_pe0, 1)
            pe.wait_ge(s_w, 14 * 16)
            for k in range(3):
                nc.tensor.transpose(ps[:, 4, k * P:(k + 1) * P], w3[:, k, :], ident[:])
            nc.tensor.transpose(ps[:, 4, 3 * P:3 * P + 4 * SKIPS], lbias_sum[:], ident[0:4 * SKIPS, 0:4 * SKIPS])\
                .then_inc(s_pe0, 1)
            pe.wait_ge(s_act0, ACT_W3T)
            mm(ps[:, 5, 0:P], w3T[:, 0, :], w3T[:, 1, :], start=True, stop=True)
            mm(ps[:, 5, P:2 * P], w3T[:, 2, :], w3[:, 3, :], start=True, stop=True).then_inc(s_pe0, 1)
            pe.wait_ge(s_dve, DV_DIFF[-1])
            gather_values(0)

            def attention_back(r):
                pe.wait_ge(s_dve, DV_ATT[r])
                for c in range(EC):
                    m = nc.tensor.transpose(ps[:, 3, c * BH + r * P:c * BH + (r + 1) * P],
                                            logit[:, r, c * P:(c + 1) * P], ident[:])
                m.then_inc(s_pe0, 1)
            attention_back(0)

            def mm3(bank, x_or_h, p, q, hi, lo, start, stop):
                w_hi, w_lo = lstm_hi[:, x_or_h, p - 1, q, :], lstm_lo[:, x_or_h, p - 1, q, :]
                mm(bank, w_hi, hi, start=start, stop=False)
                mm(bank, w_lo, hi, start=False, stop=False)
                return mm(bank, w_hi, lo, start=False, stop=stop)

            def step_l(p, i, s, c, then=None):
                n = before(p, i, s, c)
                if then and p == 1 and c == 0:
                    pe.wait_ge(c_hl, NG)
                sweep_starts = s == 0 and isinstance(i, int) and i == 0
                if sweep_starts and p == 2:
                    pe.wait_ge(l_h, 2 * (2 * i + c) + 3)
                if sweep_starts and p == 3:
                    pe.wait_ge(l_h, unit(2, i, 1, c) + 1)
                if sweep_starts and p == 4:
                    pe.wait_ge(l_h, unit(3, 2 * i + c, 2, 1) + 1)
                gates = (GATE_I, GATE_G, GATE_O) if s == 0 else (GATE_F, GATE_I, GATE_G, GATE_O)
                if s == 0:
                    until(pe, l_i, n)
                else:
                    until(pe, l_o, n)
                for q in gates:
                    if s == 0 and q == GATE_G:
                        until(pe, l_in, n)
                    if s == 0 and q == GATE_O:
                        until(pe, l_o, n)
                    m = mm3(windows(ps[:, 4 * c + GATE_BANK[q], :], p), 0, p, q, at_step(h_hi, p, i, c, s),
                            at_step(h_lo, p, i, c, s), True, s == 0)
                    if s == 0:
                        m.then_inc(l_gate[q], 1)
                if s > 0:
                    pe.wait_ge(l_h, n)
                    for q in gates:
                        mm3(ps[:, 4 * c + GATE_BANK[q], 0:cols(p)], 1, p, q, hid_hi[:, c, 0:cols(p)],
                            hid_lo[:, c, 0:cols(p)], False, True).then_inc(l_gate[q], 1)
                if then:
                    step_l(*then, 0, c)

            def starts_l(p, i):
                for c in range(2):
                    step_l(p, i, 0, c)
            pe.wait_ge(s_act0, ACT_W3P)
            pe.wait_ge(s_dve, DV_ATTT[0])
            pe.wait_ge(s_w, 14 * 16)

            def project(bank, src_s, w, sem_):
                for b in range(GRP):
                    m = mm(ps[:, bank, b * P:(b + 1) * P], src_s[:, b * P:(b + 1) * P], w, start=True, stop=True)
                m.then_inc(sem_, 1)

            def step_c(t, u):
                if active(t, 1):
                    g, k = t - 1, (u - 1) % 2
                    pe.wait_ge(c_wv, g + 1)
                    until(pe, c_ys, g)
                    for b in range(GRP):
                        for c in range(EC):
                            m = mm(ps[:, 2, b * P:(b + 1) * P], wv[k][:, c * BANK + b * P:c * BANK + (b + 1) * P],
                                   src_oh[:, c, :], start=c == 0, stop=c == EC - 1)
                    m.then_inc(c_y, 1)
                if is_step(t, 1):
                    attention_back(1)
                if active(t, 3):
                    g, k = t - 3, (u - 3) % 2
                    if is_step(t, 3):
                        pe.wait_ge(s_dve, DV_ATTT[-1])
                    pe.wait_ge(c_hs, g + 1)
                    until(pe, c_xw2s, g)
                    project(3, h1_s[k], wg[:, 1, :], c_xw2)
                if active(t, 1):
                    g, k = t - 1, (u - 1) % 2
                    pe.wait_ge(c_ys, g + 1)
                    until(pe, c_r, g)
                    project(5, y_s[k], WoutT, c_o)
                if active(t, 2):
                    g, k = t - 2, u
                    pe.wait_ge(c_xn, g + 1)
                    until(pe, c_hs, g)
                    for b in range(GRP):
                        m = nc.tensor.transpose(ps[:, 4, b * P:(b + 1) * P], xn[k][:, b * P:(b + 1) * P], ident[:])
                    m.then_inc(c_tx, 1)
                if active(t, 0) and not is_step(t, 0):
                    pe.wait_ge(c_wv, t)
                    gather_values(t)
                if active(t, 2):
                    g, k = t - 2, u
                    pe.wait_ge(c_xt, g + 1)
                    until(pe, c_xws, g)
                    project(6, x1T[k], wg[:, 0, :], c_xw)
                if active(t, 3):
                    g, k = t - 3, (u - 3) % 2
                    if is_step(t, NG + 2):
                        starts_l(1, 1)
                    pe.wait_ge(c_xw2s, g + 1)
                    until(pe, c_hl, g)
                    project(7, xw2_s[k], adjT, c_h2)
                if active(t, 2):
                    g, k = t - 2, u
                    pe.wait_ge(c_xws, g + 1)
                    pe.wait_ge(c_all, g + 1)
                    project(4, xw_s[k], adjT, c_h)
                if is_step(t, NG + 1):
                    pe.wait_ge(s_lo, 2 * SKIPS)
                    pe.wait_ge(c_r, NG)
                    pe.wait_ge(c_hs, NG)
                    starts_l(1, 0)
            run_groups(pe, step_c, 4)

            run_units(pe, starts_l, step_l)

            pe.wait_ge(l_o, UNITS_ALL)

            def transposes(bank, src_s, sem_):
                for b in range(GRP):
                    m = nc.tensor.transpose(ps[:, bank, b * P:(b + 1) * P], src_s[:, b * P:(b + 1) * P], ident[:])
                m.then_inc(sem_, 1)

            def graph_conv(bank, w_loop, src_T, neigh_s, s_neigh, n, sem_):
                mm(ps[:, bank, :], w_loop, src_T, start=True, stop=False, skip_group_check=True)
                pe.wait_ge(s_neigh, n)
                for b in range(GRP):
                    m = mm(ps[:, bank, b * P:(b + 1) * P], neigh_s[:, b * P:(b + 1) * P], adjT,
                           start=False, stop=b == GRP - 1, skip_group_check=True)
                m.then_inc(sem_, 1)

            def scores(g, k3):
                pe.wait_ge(d_qs, g + 1)
                for b in range(GRP):
                    m = mm(ps[:, 4, b * P:(b + 1) * P], q3[k3][:, b * P:(b + 1) * P],
                           x3T[k3][:, b * P:(b + 1) * P], start=True, stop=True)
                m.then_inc(d_sc, 1)

            def step_d(t, u):
                k1, k3 = (u - 1) % 2, (u - 3) % 2
                if active(t, 2):
                    g = t - 2
                    pe.wait_ge(d_h1, g + 1)
                    until(pe, d_r4, g - 2)
                    graph_conv(0, w2[:, 2, :], h1T[u], n2_s[u], d_n2s, g + 1, d_d)
                if active(t, 3):
                    g = t - 3
                    pe.wait_ge(d_x3, g + 1)
                    pe.wait_ge(d_n2s, min(g + 2, NG) if isinstance(t, int) else g + 2)
                    transposes(1, x3_s[k3], d_tx3)
                if active(t, 4):
                    g = t - 4
                    pe.wait_ge(d_p, g + 1)
                    pe.wait_ge(d_vs, g + 1)
                    transposes(3, p3[u], d_tp)
                if active(t, 1):
                    g = t - 1
                    pe.wait_ge(d_x2, g + 1)
                    until(pe, d_h1, g)
                    transposes(2, x2_s[k1], d_tx)
                if active(t, 0):
                    pe.wait_ge(d_s, t + 1)
                    until(pe, d_x2, t)
                    transposes(7, sum_s[u], d_ts)
                if active(t, 3):
                    g = t - 3
                    pe.wait_ge(d_xt3, g + 1)
                    until(pe, d_z, g)
                    mm(ps[:, 4, :], w3p[:, 0, :], x3T[k3], start=True, stop=True).then_inc(d_q, 1)
                if active(t, 4):
                    g = t - 4
                    if is_step(t, NG + 2):
                        scores(NG - 1, k3)
                    if is_step(t, NG + 3):
                        pe.wait_ge(d_r4, NG - 1)
                    pe.wait_ge(d_pt, g + 1)
                    pe.wait_ge(d_h2, min(g + 3, NG) if isinstance(t, int) else g + 3)
                    for b in range(GRP):
                        m = mm(ps[:, 0, b * P:(b + 1) * P], pT[u][:, b * P:(b + 1) * P],
                               v3[u][:, b * P:(b + 1) * P], start=True, stop=True)
                    m.then_inc(d_zz, 1)
                if active(t, 1):
                    g = t - 1
                    pe.wait_ge(d_xt, g + 1)
                    until(pe, d_n1s, g)
                    project(5, x2T[k1], w2[:, 1, :], d_n1)
                if active(t, 2):
                    g = t - 2
                    pe.wait_ge(d_u, g + 1)
                    until(pe, d_x3, g)
                    transposes(6, uT[u], d_tu)
                if active(t, 1):
                    graph_conv(2, w2[:, 0, :], x2T[k1], n1_s[k1], d_n1s, t, d_b)
                if active(t, 3):
                    if not is_step(t, NG + 2):
                        scores(t - 3, k3)
                if active(t, 3):
                    g = t - 3
                    until(pe, d_pt, g)
                    project(3, x3T[k3], w3p[:, 1, :], d_v)
                if active(t, 1):
                    g = t - 1
                    pe.wait_ge(d_h1, g + 1)
                    if active(t, 3):
                        pe.wait_ge(d_xt3, t - 2)
                    project(1, h1T[k1], w2[:, 3, :], d_n2)
            run_groups(pe, step_d, 4)

        @block.scalar
        def _(act):
            act.wait_ge(s_pe0, PE_WT)
            nc.scalar.copy(wT[:].rearrange("p k n -> p (k n)"), ps[:, 0, :]).then_inc(s_act0, 1)

            def step_a(t, u):
                if isinstance(t, int) and t % 4 == 0 and t < NG:
                    act.wait_ge(s_x[t // 4], 16)
                if is_step(t, A_ADJ):
                    for k in range(2, 4):
                        act.wait_ge(s_x[k], 16)
                if active(t, 0):
                    until(act, a_t, t - 1)
                    nc.scalar.copy(by_batch(xs[u]), grp(state, t)).then_inc(a_xs, 1)
                if active(t, 0):
                    act.wait_ge(a_t, t + 1)
                    until(act, a_qv, t - 1)
                    nc.scalar.copy(xT[u], ps[:, 0, :]).then_inc(a_xt, 1)
                if active(t, 2):
                    g, k = t - 2, u
                    act.wait_ge(a_g, g + 1)
                    until(act, a_l, g - 1)
                    nc.scalar.copy(z_s[k], ps[:, 3:5, :].rearrange("p s n -> p (s n)")).then_inc(a_z, 1)
                if is_step(t, A_ADJ):
                    act.wait_ge(s_pool, 2)
                    act.wait_ge(s_pe0, PE_ADJ)
                    nc.scalar.activation(log_adj[:], ps[:, 6, 0:E], ACT.Ln, bias=eps_col[:]).then_inc(s_act0, 1)
                    nc.scalar.copy(src_oh[:].rearrange("p c n -> p (c n)"), ps[:, 6, E:E + EC * P])\
                        .then_inc(s_act0, 1)
                for n in lstm_at_step(t):
                    act.wait_ge(s_pe0, PE_LSTM[n])
                    if n >= 2:
                        act.wait_ge(s_lo, n - 1)
                    nc.scalar.copy(lstm_t[:, n % 2, :], ps[:, 6 + n % 2, :])
                    nc.scalar.copy(lstm_hi[:, n // SKIPS, n % SKIPS].rearrange("p q h -> p (q h)"),
                                   ps[:, 6 + n % 2, :]).then_inc(s_act0, 1)
            run_groups(act, step_a, 3)

            act.wait_ge(s_pe0, PE_W3T)
            nc.scalar.copy(w3T[:].rearrange("p k n -> p (k n)"), ps[:, 4, 0:3 * P]).then_inc(s_act0, 1)
            nc.scalar.copy(lbias[:], ps[:, 4, 3 * P:3 * P + 4 * SKIPS]).then_inc(s_act0, 1)
            for r in range(RT):
                act.wait_ge(s_dve, DV_DIFF[r])
                nc.scalar.activation(fmax[:, r, :], logit[:, r, :], ACT.Exp).then_inc(s_act0, 1)
            act.wait_ge(s_pe0, PE_W3P)
            nc.scalar.copy(w3p[:].rearrange("p k n -> p (k n)"), ps[:, 5, 0:2 * P]).then_inc(s_act0, 1)

            def gates(p, i, s, c):
                n = unit(p, i, s, c)
                until(act, l_c, before(p, i, s, c))
                for q in (GATE_I, GATE_G, GATE_O) if s == 0 else (GATE_F, GATE_I, GATE_G, GATE_O):
                    if q == GATE_O and (p == 1 or is_start(p, i, s)):
                        until(act, l_hh, before(p, i, s, c))
                    act.wait_ge(l_gate[q], fgate(p, i, s, c) + 1 if q == GATE_F else n + 1)
                    a = nc.scalar.activation(gate_tile(c, q, s)[:, 0:cols(p)], ps[:, 4 * c + GATE_BANK[q], 0:cols(p)],
                                             ACT.Tanh if q == GATE_G else ACT.Sigmoid,
                                             bias=lbias[:, 4 * (p - 1) + q:4 * (p - 1) + q + 1])
                    if q == GATE_I:
                        a.then_inc(l_i, 1)
                    if q == GATE_G:
                        a.then_inc(l_in, 1)
                    if q == GATE_O:
                        a.then_inc(l_o, 1)

            def squash(p, i, s, c):
                act.wait_ge(l_c, unit(p, i, s, c) + 1)
                nc.scalar.activation(tanh_c[c][:, 0:cols(p)], cell[c][:, 0:cols(p)], ACT.Tanh).then_inc(l_tc, 1)

            def starts_l(p, i):
                for c in range(2):
                    gates(p, i, 0, c)
                for c in range(2):
                    squash(p, i, 0, c)

            def step_l(p, i, s, c, then):
                gates(p, i, s, c)
                squash(p, i, s, c)
                if then:
                    step_l(*then, 0, c, None)
            def step_c(t, u):
                if active(t, 1):
                    g, k = t - 1, (u - 1) % 2
                    act.wait_ge(c_y, g + 1)
                    until(act, c_o, g - 1)
                    nc.scalar.copy(y_s[k], ps[:, 2, :]).then_inc(c_ys, 1)
                if active(t, 2):
                    g, k = t - 2, u
                    act.wait_ge(c_tx, g + 1)
                    until(act, c_xw, g - 1)
                    nc.scalar.copy(x1T[k], ps[:, 4, :]).then_inc(c_xt, 1)
                    nc.scalar.copy(grp(x1T_all, g), by_batch(ps[:, 4, :])).then_inc(c_all, 1)
                if active(t, 3):
                    g = t - 3
                    if is_step(t, NG + 2):
                        starts_l(1, 1)
                    act.wait_ge(c_h2, g + 1)
                    nc.scalar.activation(grp(h_hi, g), by_batch(ps[:, 7, :]), ACT.Relu).then_inc(c_h2s, 1)
                if active(t, 2):
                    g, k = t - 2, u
                    act.wait_ge(c_h, g + 1)
                    until(act, c_xw2, g - 1)
                    nc.scalar.activation(h1_s[k], ps[:, 4, :], ACT.Relu).then_inc(c_hs, 1)
                if active(t, 1):
                    g, k = t - 1, (u - 1) % 2
                    act.wait_ge(c_nb, g + 1)
                    until(act, c_tx, g - 1)
                    for b in range(GRP):
                        a = nc.scalar.activation(xn[k][:, b * P:(b + 1) * P], r_s[k][:, b * P:(b + 1) * P],
                                                 ACT.Identity, bias=ln_bias[:, k, b:b + 1],
                                                 scale=rstd[:, 0, k, b:b + 1])
                    a.then_inc(c_xn, 1)
                if is_step(t, NG + 1):
                    starts_l(1, 0)
            run_groups(act, step_c, 4)

            run_units(act, starts_l, step_l)

            def step_d(t, u):
                k1, k3 = (u - 1) % 2, (u - 3) % 2
                if active(t, 2):
                    g = t - 2
                    act.wait_ge(d_d, g + 1)
                    until(act, d_u, g - 1)
                    nc.scalar.activation(h2_s[u], ps[:, 0, :], ACT.Relu, bias=half_b2[:], scale=0.5).then_inc(d_h2, 1)
                if active(t, 3):
                    g = t - 3
                    act.wait_ge(d_tx3, g + 1)
                    until(act, d_sc, g - 1)
                    nc.scalar.copy(x3T[k3], ps[:, 1, :]).then_inc(d_xt3, 1)
                if active(t, 1):
                    g = t - 1
                    act.wait_ge(d_tx, g + 1)
                    until(act, d_u, g - 1)
                    nc.scalar.copy(x2T[k1], ps[:, 2, :]).then_inc(d_xt, 1)
                if active(t, 4):
                    g = t - 4
                    act.wait_ge(d_tp, g + 1)
                    until(act, d_zz, g - 1)
                    nc.scalar.copy(pT[u], ps[:, 3, :]).then_inc(d_pt, 1)
                if active(t, 3):
                    g = t - 3
                    act.wait_ge(d_q, g + 1)
                    nc.scalar.activation(q3[k3], ps[:, 4, :], ACT.Copy, scale=SCALE).then_inc(d_qs, 1)
                if active(t, 1):
                    g = t - 1
                    act.wait_ge(d_n1, g + 1)
                    until(act, d_b, g - 1)
                    nc.scalar.copy(n1_s[k1], ps[:, 5, :]).then_inc(d_n1s, 1)
                if active(t, 1):
                    g = t - 1
                    act.wait_ge(d_b, g + 1)
                    until(act, d_d, g - 1)
                    nc.scalar.activation(h1T[k1], ps[:, 2, :], ACT.Relu, bias=b1_col[:]).then_inc(d_h1, 1)
                if active(t, 0):
                    act.wait_ge(d_nb1, t + 1)
                    until(act, d_tx, t - 1)
                    for b in range(GRP):
                        a = nc.scalar.activation(x2_s[u][:, b * P:(b + 1) * P], ps[:, 7, b * P:(b + 1) * P],
                                                 ACT.Identity, bias=ln_bias[:, u, b:b + 1],
                                                 scale=rstd[:, 0, u, b:b + 1])
                    a.then_inc(d_x2, 1)
                if active(t, 3):
                    g = t - 3
                    act.wait_ge(d_v, g + 1)
                    until(act, d_zz, g - 1)
                    nc.scalar.copy(v3[k3], ps[:, 3, :]).then_inc(d_vs, 1)
                if active(t, 1):
                    g = t - 1
                    act.wait_ge(d_n2, g + 1)
                    nc.scalar.copy(n2_s[k1], ps[:, 1, :]).then_inc(d_n2s, 1)
                if active(t, 3):
                    g = t - 3
                    act.wait_ge(d_mx, g + 1)
                    until(act, d_tp, g - 1)
                    for b in range(GRP):
                        at = bass.ds(g * GRP + b, 1)
                        a = nc.scalar.activation(p3[k3][:, b * P:(b + 1) * P], z3[k3][:, b * P:(b + 1) * P],
                                                 ACT.Exp, bias=nmax[:, at], accum_out=rowsum[:, at])
                    a.then_inc(d_p, 1)
            run_groups(act, step_d, 4)

        @block.vector
        def _(dve):
            v = nc.vector
            count = [0]

            def link(ins):
                count[0] += 1
                ins.then_inc(s_dve, 1)
                dve.wait_ge(s_dve, count[0])

            dve.wait_ge(s_idx, 4 * 16)
            dve.wait_ge(s_pool, 1)
            link(v.tensor_copy(idx_row[:].rearrange("p k e -> p (k e)"), idx_row_i[:].rearrange("p k e -> p (k e)")))
            link(v.tensor_copy(idx_col[:].rearrange("p k c -> p (k c)"), idx_col_i[:].rearrange("p k c -> p (k c)")))
            link(v.scalar_tensor_tensor(out=key_row[:], in0=idx_row[:, 0, :], scalar=float(E), in1=e_row[:],
                                        op0=ALU.mult, op1=ALU.add))
            link(v.scalar_tensor_tensor(out=key_col[:], in0=idx_col[:, 0, :], scalar=float(E), in1=e_col[:],
                                        op0=ALU.mult, op1=ALU.add))
            for c in range(EC):
                link(v.tensor_scalar(perm[:, c, :], key_row[:], key_col[:, c:c + 1], None, ALU.is_lt, ALU.add,
                                     accum_out=rank[:, c:c + 1]))
            dve.wait_ge(s_pool, 2)
            for c in range(EC):
                link(v.tensor_scalar(perm[:, c, :], e_row[:], rank[:, c:c + 1], None, ALU.is_equal))
                for k in range(2):
                    link(v.tensor_scalar(idx_wide[:, k, c, :], ones[:], idx_col[:, k, c:c + 1], None, ALU.mult))
            assert count[0] == DV_PERM
            dve.wait_ge(s_pe0, PE_SORTED)
            link(v.tensor_copy(sorted_row[:].rearrange("p k e -> p (k e)"), ps[:, 6, :]))
            link(v.tensor_scalar(srcT[:], sorted_row[:, 0, :], e_col[:, 0:1], None, ALU.is_equal))
            link(v.tensor_scalar(dstT[:], sorted_row[:, 1, :], e_col[:, 0:1], None, ALU.is_equal))
            link(v.tensor_tensor(endsT[:], srcT[:], dstT[:], ALU.add))
            assert count[0] == DV_ONEHOT
            dve.wait_ge(s_pool, POOL_CONST)
            dve.wait_ge(s_early, 5 * 16)
            link(v.tensor_scalar(a_heads[:], head_of[:], a_col[:], None, ALU.mult))
            assert count[0] == DV_HEADS

            def step_a(t, u):
                if active(t, 1):
                    g, k = t - 1, (u - 1) % 2
                    dve.wait_ge(a_qv, g + 1)
                    until(dve, a_g, g - 1)
                    qv = ps[:, 1:3, :].rearrange("p s (b w n) -> p (s b) w n", b=GRP // 2, w=2)
                    q, val = qv[:, :, 0, :], qv[:, :, 1, :]
                    v.tensor_copy(by_batch(q_hi[:, k, :]), q)
                    v.tensor_copy(grp(v_hi, g), val).then_inc(a_hi, 1)
                    dve.wait_ge(a_hi, g + 1)
                    v.tensor_tensor(by_batch(q_lo[:, k, :]), q, by_batch(q_hi[:, k, :]), ALU.subtract).then_inc(a_q, 1)
                    v.tensor_tensor(grp(v_lo, g), val, grp(v_hi, g), ALU.subtract).then_inc(a_v, 1)
                if active(t, 2):
                    g, k = t - 2, u
                    dve.wait_ge(a_z, g + 1)
                    until(dve, a_e, g - 1)
                    v.scalar_tensor_tensor(out=l_s[k], in0=z_s[k], scalar=LRELU_SLOPE,
                                           in1=ps[:, 3:5, :].rearrange("p s n -> p (s n)"),
                                           op0=ALU.mult, op1=ALU.max).then_inc(a_l, 1)
                if is_step(t, A_PICK):
                    link(v.tensor_tensor(same[:, 1:E], sorted_row[:, 0, 1:E], sorted_row[:, 0, 0:E - 1], ALU.is_equal))
                    link(v.tensor_scalar(reset[:], same[:], -1.0, RESET, ALU.add, ALU.mult))
                    link(v.tensor_scalar(last[:], same[:, 1:E + 1], -1.0, 1.0, ALU.mult, ALU.add))
                    dve.wait_ge(s_pe0, PE_PICK)
                    link(v.tensor_tensor(adj_pick[:], ps[:, 7, 0:E], dstT[:], ALU.mult))
                    assert count[0] == DV_PICK
                if is_step(t, A_ADJ):
                    dve.wait_ge(s_w, 14 * 16)
                    link(v.tensor_tensor(lbias_sum[:], lbias_nat[:, 0, :], lbias_nat[:, 1, :], ALU.add))
                    link(v.tensor_scalar(half_b2[:], b2_col[:], 0.5, None, ALU.mult))
                    assert count[0] == DV_BIAS
            run_groups(dve, step_a, 3)

            dve.wait_ge(a_e, NG)
            link(v.tensor_copy(e_s, ps[:, 5, :]))
            assert count[0] == DV_LOGIT
            dve.wait_ge(s_pe0, PE_LOGIT)
            dve.wait_ge(s_act0, ACT_LOG)
            for r in range(RT):
                link(v.tensor_tensor(logit[:, r, :], ps[:, 0, r * E:(r + 1) * E], log_adj[:], ALU.add))
                link(v.tensor_tensor_scan(fmax[:, r, :], reset[:, 0:E], logit[:, r, :], 0.0, ALU.add, ALU.max))
                link(v.tensor_tensor_scan(bmax[:, r, ::-1], reset[:, 1:E + 1][:, ::-1], fmax[:, r, ::-1], 0.0,
                                          ALU.add, ALU.max))
                link(v.tensor_tensor(logit[:, r, :], logit[:, r, :], bmax[:, r, :], ALU.subtract))
                assert count[0] == DV_DIFF[r]

            def attention(r):
                dve.wait_ge(s_act0, ACT_EXP[r])
                link(v.tensor_tensor_scan(bmax[:, r, :], same[:, 0:E], fmax[:, r, :], 0.0, ALU.mult, ALU.add))
                link(v.tensor_tensor(bmax[:, r, :], bmax[:, r, :], last[:], ALU.mult))
                link(v.tensor_tensor_scan(logit[:, r, ::-1], same[:, 1:E + 1][:, ::-1], bmax[:, r, ::-1], 0.0,
                                          ALU.mult, ALU.add))
                link(v.reciprocal(bmax[:, r, :], logit[:, r, :]))
                link(v.tensor_tensor(logit[:, r, :], fmax[:, r, :], bmax[:, r, :], ALU.mult))
                assert count[0] == DV_ATT[r]

            def attention_copy(r):
                dve.wait_ge(s_pe0, PE_ATT[r])
                link(v.tensor_copy(attT[:, :, r * P:(r + 1) * P],
                                   ps[:, 3, :].rearrange("p (c n) -> p c n", c=EC)[:, :, r * P:(r + 1) * P]))
                assert count[0] == DV_ATTT[r]
            attention(0)
            attention_copy(0)

            def ln_moments(j, src_b, buf, n, s_mv, s_ve, minus_mean=None):
                for b in range(GRP):
                    v.bn_stats(stats[:, j, buf, b, :], src_b[:, b * P:(b + 1) * P])
                dve.drain()
                for b in range(GRP):
                    m = v.bn_aggr(moments[:, j, buf, b, :], stats[:, j, buf, b, :])
                m.then_inc(s_mv, 1)
                dve.wait_ge(s_mv, n)
                if minus_mean is not None:
                    v.tensor_scalar(minus_mean, moments[:, j, buf, :, 0], -1.0, None, ALU.mult)
                v.tensor_scalar(var_eps[:, j, buf, :], moments[:, j, buf, :, 1], LN_EPS, None,
                                ALU.add).then_inc(s_ve, 1)

            def ln_scale(j, dst_b, src_b, buf, n, s_rs, s_out):
                dve.wait_ge(s_rs, n)
                for b in range(GRP):
                    m = v.tensor_scalar(dst_b[:, b * P:(b + 1) * P], src_b[:, b * P:(b + 1) * P],
                                        moments[:, j, buf, b, 0:1], rstd[:, j, buf, b:b + 1],
                                        ALU.subtract, ALU.mult)
                m.then_inc(s_out, 1)

            def moments_1(t, u):
                dve.wait_ge(d_ts, t + 1)
                ln_moments(0, ps[:, 7, :], u, t + 1, d_mv1, d_ve1, nmean[:, u, :])

            def new_cell(p, i, s, c):
                n, w = unit(p, i, s, c), cols(p)
                gi, gf, gg = (gate_s[c][q][:, 0:w] for q in (GATE_I, GATE_F, GATE_G))
                cc = cell[c][:, 0:w]
                dve.wait_ge(l_in, n + 1)
                if s == 0:
                    v.tensor_tensor(cc, gi, gg, ALU.mult).then_inc(l_c, 1)
                else:
                    f = fgate(p, i, s, c)
                    v.tensor_tensor(gi, gi, gg, ALU.mult)
                    v.tensor_tensor(gf, gf, cc, ALU.mult).then_inc(l_fc, 1)
                    dve.wait_ge(l_fc, f + 1)
                    v.tensor_tensor(cc, gi, gf, ALU.add).then_inc(l_c, 1)

            def hidden_parts(p, s, c, i):
                if s < p - 1:
                    w = cols(p)
                    return hid[c][:, 0:w], hid_hi[:, c, 0:w], hid_lo[:, c, 0:w]
                return windows(hid[c], p), at_step(h_hi, p, i, c, s), at_step(h_lo, p, i, c, s)

            def new_hidden(p, i, s, c):
                n, w = unit(p, i, s, c), cols(p)
                h, hi, lo = hidden_parts(p, s, c, i)
                gate_o, tc = gate_tile(c, GATE_O, s), tanh_c[c]
                gate_o, tc = (ap[:, 0:w] if s < p - 1 else windows(ap, p) for ap in (gate_o, tc))
                dve.wait_ge(l_tc, n + 1)
                dve.wait_ge(l_o, n + 1)
                until(dve, l_h, before(p, i, s, c))
                v.tensor_tensor(hi, gate_o, tc, ALU.mult)
                v.tensor_tensor(h, gate_o, tc, ALU.mult).then_inc(l_hh, 1)

            def low_part(p, i, s, c):
                h, hi, lo = hidden_parts(p, s, c, i)
                dve.wait_ge(l_hh, unit(p, i, s, c) + 1)
                v.tensor_tensor(lo, h, hi, ALU.subtract).then_inc(l_h, 1)

            def starts_l(p, i):
                for unit_part in (new_cell, new_hidden):
                    for c in range(2):
                        unit_part(p, i, 0, c)

            def step_l(p, i, s, c, then):
                new_cell(p, i, s, c)
                if p == SKIPS and s == p - 1 and c == 1 and not then:
                    moments_1(0, 0)
                if p == 1 and c == 0:
                    dve.wait_ge(l_h, 2 * (PAIRS[1] - 1))
                new_hidden(p, i, s, c)
                if then:
                    new_cell(*then, 0, c)
                low_part(p, i, s, c)
                if then:
                    new_hidden(*then, 0, c)
                    low_part(*then, 0, c)
            dve.wait_ge(s_lo, 2 * SKIPS)

            def step_c(t, u):
                if active(t, 4):
                    g = t - 4
                    dve.wait_ge(c_h2s, g + 1)
                    v.scalar_tensor_tensor(out=grp(h_lo, g), in0=by_batch(ps[:, 7, :]), scalar=0.0, in1=grp(h_hi, g),
                                           op0=ALU.max, op1=ALU.subtract).then_inc(c_hl, 1)
                if active(t, 3):
                    g, k = t - 3, (u - 3) % 2
                    dve.wait_ge(c_xw2, g + 1)
                    until(dve, c_h2, g - 1)
                    v.tensor_tensor(by_batch(xw2_s[k]), by_batch(ps[:, 3, :]), per_batch_row(bg[:, 1, :]),
                                    ALU.add).then_inc(c_xw2s, 1)
                if active(t, 1):
                    g, k = t - 1, (u - 1) % 2
                    dve.wait_ge(c_o, g + 1)
                    v.tensor_tensor(by_batch(r_s[k]), by_batch(ps[:, 5, :]), grp(state, g), ALU.add).then_inc(c_r, 1)
                    dve.wait_ge(c_r, g + 1)
                    ln_moments(0, r_s[k], k, g + 1, c_mv, c_ve, nmean[:, k, :])
                if active(t, 2):
                    g, k = t - 2, u
                    dve.wait_ge(c_xw, g + 1)
                    until(dve, c_h, g - 1)
                    v.tensor_tensor(by_batch(xw_s[k]), by_batch(ps[:, 6, :]), per_batch_row(bg[:, 0, :]),
                                    ALU.add).then_inc(c_xws, 1)
                if active(t, 0):
                    dve.wait_ge(c_vd, t + 1)
                    until(dve, c_y, t - 1)
                    for c in range(EC):
                        m = v.tensor_tensor(
                            wv[u][:, c * BANK:(c + 1) * BANK].rearrange("p (h d) -> p h d", h=GH),
                            ps[:, c, :].rearrange("p (h d) -> p h d", h=GH),
                            attT[:, c, bass.ds(t * GH, GH)].rearrange("p (h o) -> p h o", o=1)
                            .broadcast_to([P, GH, DH]), ALU.mult)
                    m.then_inc(c_wv, 1)
                if is_step(t, 0):
                    attention(1)
                if is_step(t, 1):
                    attention_copy(1)
                if is_step(t, NG + 1):
                    starts_l(1, 0)
                if is_step(t, NG + 2):
                    starts_l(1, 1)
            run_groups(dve, step_c, 4)

            run_units(dve, starts_l, step_l)

            def masked_scores(g, k3):
                dve.wait_ge(d_sc, g + 1)
                until(dve, d_p, g - 1)
                v.tensor_tensor(by_batch(z3[k3]), by_batch(ps[:, 4, :]), per_batch_row(mask[:]),
                                ALU.add).then_inc(d_z, 1)
                dve.wait_ge(d_z, g + 1)
                v.tensor_reduce(nmax[:, bass.ds(g * GRP, GRP)], by_batch(z3[k3]), AX_X, ALU.max,
                                negate=True).then_inc(d_mx, 1)

            def x3_rows(g, u):
                until(dve, d_tx3, g - 1)
                ln_scale(1, x3_s[u], ps[:, 6, :], u, g + 1, d_rs2, d_x3)

            def step_d(t, u):
                k3 = (u - 3) % 2
                if active(t, 2):
                    g = t - 2
                    dve.wait_ge(d_h2, g + 1)
                    until(dve, d_tu, g - 1)
                    v.scalar_tensor_tensor(out=uT[u], in0=x2T[u], scalar=1.5, in1=h2_s[u],
                                           op0=ALU.mult, op1=ALU.add).then_inc(d_u, 1)
                if active(t, 0):
                    if not is_step(t, 0):
                        moments_1(t, u)
                if active(t, 4):
                    g = t - 4
                    if is_step(t, NG + 2):
                        masked_scores(NG - 1, k3)
                    dve.wait_ge(d_p, g + 1)
                    v.reciprocal(rinv[:, bass.ds(g * GRP, GRP)], rowsum[:, bass.ds(g * GRP, GRP)]).then_inc(d_ri, 1)
                    dve.wait_ge(d_ri, g + 1)
                    dve.wait_ge(d_zz, g + 1)
                    for b in range(GRP):
                        m = v.scalar_tensor_tensor(
                            out=r3_s[u][:, b * P:(b + 1) * P], in0=ps[:, 0, b * P:(b + 1) * P],
                            scalar=rinv[:, bass.ds(g * GRP + b, 1)], in1=x3_s[u][:, b * P:(b + 1) * P],
                            op0=ALU.mult, op1=ALU.add)
                    m.then_inc(d_r4, 1)
                    dve.wait_ge(d_r4, g + 1)
                    ln_moments(2, r3_s[u], u, g + 1, d_mv3, d_ve3)
                if active(t, 2):
                    g = t - 2
                    dve.wait_ge(d_tu, g + 1)
                    ln_moments(1, ps[:, 6, :], u, g + 1, d_mv2, d_ve2)
                if active(t, 3):
                    if not is_step(t, NG + 2):
                        masked_scores(t - 3, k3)
                if active(t, 2):
                    g = t - 2
                    until(dve, d_tx3, g - 1)
                    ln_scale(1, x3_s[u], ps[:, 6, :], u, g + 1, d_rs2, d_x3)
                if active(t, 4):
                    g = t - 4
                    if not isinstance(g, int) or g >= 2:
                        dve.wait_ge(d_out[u], (g - u) * 8)
                    ln_scale(2, o_s[u], r3_s[u], u, g + 1, d_rs3, d_o)
            run_groups(dve, step_d, 4)


_INS = ["x", "adj", "L0_gnn_W_lin", "L0_gnn_W_val", "L0_gnn_a", "L0_gnn_W_out", "L0_gnn_src", "L0_gnn_dst",
        "L1_gnn_Wg0", "L1_gnn_bg0", "L1_gnn_Wg1", "L1_gnn_bg1", "L1_gnn_Wih", "L1_gnn_Whh", "L1_gnn_bih",
        "L1_gnn_bhh", "L2_gnn_w1_loop", "L2_gnn_w1_neigh", "L2_gnn_b1", "L2_gnn_w2_loop", "L2_gnn_w2_neigh",
        "L2_gnn_b2", "L3_gnn_Wqkv", "L3_gnn_Wo"]


def kernel(**inputs):
    import numpy as _np
    import concourse.bacc as _bacc
    from concourse import mybir as _mybir
    from concourse.bass_utils import run_bass_kernel_spmd as _run

    nc = _bacc.Bacc("TRN2", target_bir_lowering=False, num_devices=1)
    arrays, args = {}, []
    for name in _INS:
        a = _np.ascontiguousarray(inputs[name])
        arrays[f"in_{name}"] = a
        args.append(nc.dram_tensor(f"in_{name}", a.shape, _mybir.dt.from_np(a.dtype), kind="ExternalInput").ap())
    out = nc.dram_tensor("out_x", arrays["in_x"].shape, _mybir.dt.from_np(_np.dtype("float32")),
                         kind="ExternalOutput").ap()
    build(nc, *args, out)
    r = _run(nc, [arrays], core_ids=[0])
    return r.results[0]["out_x"]
```
